# Optimizing a Trainium2 kernel written in Bass

```python
import numpy as np
import jax
import jax.numpy as jnp

def _softmax(x, axis=-1):
    return jax.nn.softmax(x, axis=axis)

def _gelu(x):
    return jax.nn.gelu(x, approximate=True)

def _silu(x):
    return jax.nn.silu(x)

def _sigmoid(x):
    return jax.nn.sigmoid(x)

def _layernorm(x, axis=-1, eps=1e-05):
    m = jnp.mean(x, axis=axis, keepdims=True)
    v = jnp.var(x, axis=axis, keepdims=True)
    return (x - m) / jnp.sqrt(v + eps)

def _scatter_add(tgt, idx, src, axis=0):
    return tgt.at[idx].add(src)

def _segment_sum(src, seg, n):
    return jax.ops.segment_sum(src, seg, n)
kernel_name = 'mk_decoder_postln_d1_seqx_r8_298774'

def setup_inputs(seed: int=0):
    np.random.seed(seed)
    _w = jnp.asarray

    def _rec_inputs():
        import jax
        import jax.numpy as jnp
        _rk = jax.random.key(seed)
        x = -0.0002928 + 1 * jax.random.normal(jax.random.fold_in(_rk, 1), (8, 256, 128), jnp.float32)
        _lenS = 256 - jax.random.randint(jax.random.fold_in(_rk, 7), (8,), 0, max(1, 256 // 4) + 1, jnp.int32)
        _lenS2 = 64 - jax.random.randint(jax.random.fold_in(_rk, 8), (8,), 0, max(1, 64 // 4) + 1, jnp.int32)
        _ctx_1024P = jax.random.normal(jax.random.fold_in(_rk, 11), (8, 16, 128), jnp.float32)
        _ctx_1024c = jax.random.dirichlet(jax.random.fold_in(_rk, 511), 0.3 * jnp.ones((16,), jnp.float32), (8, 64))
        _ctx_1024t = jnp.einsum('bsk,bkd->bsd', _ctx_1024c, _ctx_1024P)
        _ctx_1024t = _ctx_1024t * jax.lax.rsqrt(jnp.mean(jnp.square(_ctx_1024t)) + 1e-12) * 0.953939
        ctx_1024 = -1.39393e-06 + 0.999914 * (_ctx_1024t + 0.3 * jax.random.normal(jax.random.fold_in(_rk, 611), (8, 64, 128), jnp.float32))
        _validS = jnp.arange(256)[None, :] < _lenS[:, None]
        _validS2 = jnp.arange(64)[None, :] < _lenS2[:, None]
        _causal = jnp.tril(jnp.ones((256, 256), dtype=bool))
        mask_SxS2_bk0 = jnp.logical_not(jnp.broadcast_to(_validS2[0:1, :], (256, 64)))
        return (x, ctx_1024, mask_SxS2_bk0)
    x, ctx_1024, mask_SxS2_bk0 = _rec_inputs()

    def _L0_attn_setup():
        import jax, jax.numpy as jnp
        import numpy as np
        B, S, D, H, R = (8, 128, 128, 8, 32)
        DH = D // H

        def _lowrank(xh, U, V, b):
            t = jnp.einsum('bshd,hrd->bshr', xh, V)
            return jnp.einsum('bshr,hdr->bshd', t, U) + b
        key = jax.random.key(seed)
        ks = jax.random.split(key, 10)
        p = lambda k, shape: jax.random.normal(k, shape, dtype=jnp.float32) * 0.02
        return {'x': jax.random.normal(ks[0], (B, S, D), dtype=jnp.float32), 'Uq': p(ks[1], (H, DH, R)), 'Vq': p(ks[2], (H, R, DH)), 'bq': p(ks[3], (H, DH)), 'Uk': p(ks[4], (H, DH, R)), 'Vk': p(ks[5], (H, R, DH)), 'bk': p(ks[6], (H, DH)), 'Uv': p(ks[7], (H, DH, R)), 'Vv': p(ks[8], (H, R, DH)), 'bv': p(ks[9], (H, DH))}
    _L0_attn_all = _L0_attn_setup()
    _L0_attn_in = {k: v for k, v in _L0_attn_all.items() if k in ('Uq', 'Vq', 'bq', 'Uk', 'Vk', 'bk', 'Uv', 'Vv', 'bv')}
    del _L0_attn_all

    def _L0_xattn_setup():
        import jax, jax.numpy as jnp
        import numpy as np
        D_MODEL = 128
        N_HEADS = 16
        HEAD_DIM = D_MODEL // N_HEADS
        B, SQ, SK = (2, 256, 256)

        def _split_heads(x):
            b, s, _ = x.shape
            return x.reshape(b, s, N_HEADS, HEAD_DIM).transpose(0, 2, 1, 3)
        key = jax.random.key(seed)
        ks = jax.random.split(key, 12)
        init = 0.02
        inp = {'queries': jax.random.normal(ks[0], (B, SQ, D_MODEL), jnp.float32), 'keys': jax.random.normal(ks[1], (B, SK, D_MODEL), jnp.float32), 'values': jax.random.normal(ks[2], (B, SK, D_MODEL), jnp.float32), 'Wq': jax.random.normal(ks[3], (D_MODEL, D_MODEL), jnp.float32) * init, 'bq': jnp.zeros((D_MODEL,), jnp.float32), 'Wk': jax.random.normal(ks[4], (D_MODEL, D_MODEL), jnp.float32) * init, 'bk': jnp.zeros((D_MODEL,), jnp.float32), 'Wv': jax.random.normal(ks[5], (D_MODEL, D_MODEL), jnp.float32) * init, 'bv': jnp.zeros((D_MODEL,), jnp.float32), 'Wo': jax.random.normal(ks[6], (D_MODEL, D_MODEL), jnp.float32) * init, 'bo': jnp.zeros((D_MODEL,), jnp.float32), 'mask': jnp.tril(jnp.ones((SQ, SK), dtype=bool))}
        return inp
    _L0_xattn_all = _L0_xattn_setup()
    _L0_xattn_in = {k: v for k, v in _L0_xattn_all.items() if k in ('Wq', 'bq', 'Wk', 'bk', 'Wv', 'bv', 'Wo', 'bo')}
    del _L0_xattn_all

    def _L0_ffn_setup():
        import jax, jax.numpy as jnp
        import numpy as np
        D, H, E, K, S = (128, 256, 8, 2, 1)
        B, L = (4, 256)
        key = jax.random.key(seed)
        ks = jax.random.split(key, 9)
        std = 0.02
        return {'x': jax.random.normal(ks[0], (B, L, D), dtype=jnp.float32), 'router_w': jax.random.normal(ks[1], (E, D), dtype=jnp.float32) * std, 'experts_bias': jnp.zeros((E,), dtype=jnp.float32), 'w1': jax.random.normal(ks[2], (E, D, H), dtype=jnp.float32) * std, 'w3': jax.random.normal(ks[3], (E, D, H), dtype=jnp.float32) * std, 'w2': jax.random.normal(ks[4], (E, H, D), dtype=jnp.float32) * std, 'sw1': jax.random.normal(ks[5], (S, D, H), dtype=jnp.float32) * std, 'sw3': jax.random.normal(ks[6], (S, D, H), dtype=jnp.float32) * std, 'sw2': jax.random.normal(ks[7], (S, H, D), dtype=jnp.float32) * std}
    _L0_ffn_all = _L0_ffn_setup()
    _L0_ffn_in = {k: v for k, v in _L0_ffn_all.items() if k in ('router_w', 'experts_bias', 'w1', 'w3', 'w2', 'sw1', 'sw3', 'sw2')}
    del _L0_ffn_all
    return {'x': x, 'ctx_1024': ctx_1024, 'mask_SxS2_bk0': mask_SxS2_bk0, 'L0_attn_Uq': _L0_attn_in['Uq'], 'L0_attn_Vq': _L0_attn_in['Vq'], 'L0_attn_bq': _L0_attn_in['bq'], 'L0_attn_Uk': _L0_attn_in['Uk'], 'L0_attn_Vk': _L0_attn_in['Vk'], 'L0_attn_bk': _L0_attn_in['bk'], 'L0_attn_Uv': _L0_attn_in['Uv'], 'L0_attn_Vv': _L0_attn_in['Vv'], 'L0_attn_bv': _L0_attn_in['bv'], 'L0_xattn_Wq': _L0_xattn_in['Wq'], 'L0_xattn_bq': _L0_xattn_in['bq'], 'L0_xattn_Wk': _L0_xattn_in['Wk'], 'L0_xattn_bk': _L0_xattn_in['bk'], 'L0_xattn_Wv': _L0_xattn_in['Wv'], 'L0_xattn_bv': _L0_xattn_in['bv'], 'L0_xattn_Wo': _L0_xattn_in['Wo'], 'L0_xattn_bo': _L0_xattn_in['bo'], 'L0_ffn_router_w': _L0_ffn_in['router_w'], 'L0_ffn_experts_bias': _L0_ffn_in['experts_bias'], 'L0_ffn_w1': _L0_ffn_in['w1'], 'L0_ffn_w3': _L0_ffn_in['w3'], 'L0_ffn_w2': _L0_ffn_in['w2'], 'L0_ffn_sw1': _L0_ffn_in['sw1'], 'L0_ffn_sw3': _L0_ffn_in['sw3'], 'L0_ffn_sw2': _L0_ffn_in['sw2']}

def reference(x, ctx_1024, mask_SxS2_bk0, L0_attn_Uq, L0_attn_Vq, L0_attn_bq, L0_attn_Uk, L0_attn_Vk, L0_attn_bk, L0_attn_Uv, L0_attn_Vv, L0_attn_bv, L0_xattn_Wq, L0_xattn_bq, L0_xattn_Wk, L0_xattn_bk, L0_xattn_Wv, L0_xattn_bv, L0_xattn_Wo, L0_xattn_bo, L0_ffn_router_w, L0_ffn_experts_bias, L0_ffn_w1, L0_ffn_w3, L0_ffn_w2, L0_ffn_sw1, L0_ffn_sw3, L0_ffn_sw2):
    import jax
    import jax.numpy as jnp

    def _L0_attn_ref(x, Uq, Vq, bq, Uk, Vk, bk, Uv, Vv, bv):
        import jax, jax.numpy as jnp
        import numpy as np
        B, S, D, H, R = (8, 128, 128, 8, 32)
        DH = D // H

        def _lowrank(xh, U, V, b):
            t = jnp.einsum('bshd,hrd->bshr', xh, V)
            return jnp.einsum('bshr,hdr->bshd', t, U) + b
        b_, s_, _ = x.shape
        xh = x.reshape(b_, s_, H, DH)
        q = _lowrank(xh, Uq, Vq, bq)
        k = _lowrank(xh, Uk, Vk, bk)
        v = _lowrank(xh, Uv, Vv, bv)
        scores = jnp.einsum('bqhd,bkhd->bhqk', q, k) / DH ** 0.5
        attn = jax.nn.softmax(scores, axis=-1)
        out = jnp.einsum('bhqk,bkhd->bqhd', attn, v)
        return out.reshape(b_, s_, D)

    def _L0_xattn_ref(queries, keys, values, Wq, bq, Wk, bk, Wv, bv, Wo, bo, mask):
        import jax, jax.numpy as jnp
        import numpy as np
        D_MODEL = 128
        N_HEADS = 16
        HEAD_DIM = D_MODEL // N_HEADS
        B, SQ, SK = (2, 256, 256)

        def _split_heads(x):
            b, s, _ = x.shape
            return x.reshape(b, s, N_HEADS, HEAD_DIM).transpose(0, 2, 1, 3)
        q = _split_heads(queries @ Wq + bq)
        k = _split_heads(keys @ Wk + bk)
        v = _split_heads(values @ Wv + bv)
        scale = 1.0 / np.sqrt(HEAD_DIM).astype(np.float32)
        scores = jnp.einsum('bhqd,bhkd->bhqk', q, k) * scale
        neg = jnp.finfo(scores.dtype).min
        scores = jnp.where(mask[None, None, :, :], scores, neg)
        probs = jax.nn.softmax(scores, axis=-1)
        out = jnp.einsum('bhqk,bhkd->bhqd', probs, v)
        b, h, sq, hd = out.shape
        out = out.transpose(0, 2, 1, 3).reshape(b, sq, h * hd)
        return out @ Wo + bo

    def _L0_ffn_ref(x, router_w, experts_bias, w1, w3, w2, sw1, sw3, sw2):
        import jax, jax.numpy as jnp
        import numpy as np
        D, H, E, K, S = (128, 256, 8, 2, 1)
        B, L = (4, 256)
        b, l, d = x.shape
        xf = x.reshape(-1, d)
        sg = jnp.einsum('td,sdh->tsh', xf, sw1)
        su = jnp.einsum('td,sdh->tsh', xf, sw3)
        shared_out = jnp.einsum('tsh,shd->td', jax.nn.silu(sg) * su, sw2)
        logits = xf @ router_w.T + experts_bias
        rw, sel = jax.lax.top_k(logits, K)
        rw = jax.nn.softmax(rw.astype(jnp.float32), axis=-1).astype(x.dtype)
        cw = (jax.nn.one_hot(sel, E, dtype=x.dtype) * rw[..., None]).sum(axis=1)
        g = jnp.einsum('td,edh->teh', xf, w1)
        u = jnp.einsum('td,edh->teh', xf, w3)
        eo = jax.nn.silu(g) * u
        moe_out = jnp.einsum('te,teh,ehd->td', cw, eo, w2)
        return (moe_out + shared_out).reshape(b, l, d)
    x = _layernorm(x + _L0_attn_ref(x, L0_attn_Uq, L0_attn_Vq, L0_attn_bq, L0_attn_Uk, L0_attn_Vk, L0_attn_bk, L0_attn_Uv, L0_attn_Vv, L0_attn_bv), axis=-1)
    x = _layernorm(x + _L0_xattn_ref(x, ctx_1024, ctx_1024, L0_xattn_Wq, L0_xattn_bq, L0_xattn_Wk, L0_xattn_bk, L0_xattn_Wv, L0_xattn_bv, L0_xattn_Wo, L0_xattn_bo, mask_SxS2_bk0), axis=-1)
    x = _layernorm(x + _L0_ffn_ref(x, L0_ffn_router_w, L0_ffn_experts_bias, L0_ffn_w1, L0_ffn_w3, L0_ffn_w2, L0_ffn_sw1, L0_ffn_sw3, L0_ffn_sw2), axis=-1)
    return x

_drawn_inputs = setup_inputs


def setup_inputs(seed=0):
    import zlib

    import numpy as np

    out = dict(_drawn_inputs(seed))
    spreads = {'L0_xattn_bq': (0.0, 0.8),
     'L0_xattn_bk': (0.0, 0.8),
     'L0_xattn_bv': (0.0, 0.36),
     'L0_xattn_bo': (0.0, 0.1),
     'L0_ffn_experts_bias': (0.0, 0.8)}
    factors = {'L0_attn_Uq': 8.0,
     'L0_attn_Vq': 8.0,
     'L0_attn_bq': 8.0,
     'L0_attn_Uk': 8.0,
     'L0_attn_Vk': 8.0,
     'L0_attn_Uv': 8.0,
     'L0_attn_Vv': 8.0,
     'L0_xattn_Wq': 8.0,
     'L0_xattn_Wk': 8.0,
     'L0_ffn_router_w': 8.0,
     'L0_ffn_w1': 8.0,
     'L0_ffn_w3': 8.0,
     'L0_ffn_w2': 8.0,
     'L0_ffn_sw1': 6.958,
     'L0_ffn_sw3': 6.877,
     'L0_ffn_sw2': 6.887}
    for name, (base, spread) in spreads.items():
        noise = np.random.default_rng([zlib.crc32(name.encode()), seed]).standard_normal(out[name].shape)
        drawn = base * np.exp(spread * noise) if base else spread * noise
        out[name] = jnp.asarray(drawn.astype(out[name].dtype))
    for name, factor in factors.items():
        out[name] = (out[name] * factor).astype(out[name].dtype)
    return out
```

```python
from contextlib import ExitStack

import concourse.bass as bass
from concourse import mybir
from concourse.alu_op_type import AluOpType as ALU

F32 = mybir.dt.float32
F32R = mybir.dt.float32r
BF16 = mybir.dt.bfloat16
U32 = mybir.dt.uint32
U8 = mybir.dt.uint8
ACT = mybir.ActivationFunctionType
AX_X = mybir.AxisListType.X

P = 128
B, S, D = 8, 256, 128
QT = S // P
NT = B * QT
H1, DH1, R1 = 8, 16, 32
H2, DH2, SK = 16, 8, 64
PAIRS = H2 // 2
E, HF = 8, 256
CH = HF // P
GT = 512
NG = B * S // GT
GQ = GT // P
NE = E + 1
EPS = 1e-5
SCALE1 = 1.0 / DH1 ** 0.5
SCALE2 = 1.0 / DH2 ** 0.5
MASKED = -(2.0 ** 100)

TERMS = [3, 2, 1]
NTERM = sum(TERMS)
K1 = NTERM * DH1
M1 = K1
K1M = K1 + 2
C2 = SK
K2 = SK + NTERM * DH2
K2M = K2 + 2

ROUTE_GAP = 2 * NT + 3
SPLIT_STEPS = 3
LN_STEPS = 9
LN_STATS = 7
LN3_STEPS = 3 * GQ
STAGES = 5
FIRST_FULL, LAST_FULL = STAGES, B - 1
N_STEPS = B + STAGES - 1


def pipeline(eng, step):
    def at(s):
        return [s - k if 0 <= s - k < B else None for k in range(STAGES)]

    for s in range(FIRST_FULL):
        step(at(s))
    with eng.Fori(FIRST_FULL, LAST_FULL + 1) as s:
        step([s - k for k in range(STAGES)])
    for s in range(LAST_FULL + 1, N_STEPS):
        step(at(s))


def on(b):
    return b is not None


def last_step(b4):
    return isinstance(b4, int) and b4 == B - 1


def wait_alone(eng, sem, value, carrier):
    eng.wait_ge(sem, value)
    if not isinstance(value, int):
        eng.sem_inc(carrier, 1)


def decoder_kernel(nc, t):
    ctx = ExitStack()
    with ctx:
        def sb(name, shape, dt=F32):
            return ctx.enter_context(nc.sbuf_tensor(name, shape, dt))

        def pb(name, shape, dt=F32):
            return ctx.enter_context(nc.psum_tensor(name, shape, dt))

        def sem(name):
            return ctx.enter_context(nc.semaphore(name))

        ident = sb("ident", [P, P])
        identb = sb("identb", [P, P], BF16)
        headmask = sb("headmask", [P, 2, H1])
        lowV = sb("lowV", [P, 3, 2, DH1])
        lowU = sb("lowU", [P, 3, 2, DH1])
        wqkv = sb("wqkv", [P, 3, P])
        bqk = sb("bqk", [P, 2])
        bvB = sb("bvB", [P, P])
        boB = sb("boB", [P, P])
        wx = sb("wx", [P, 4, P])
        bx = sb("bx", [P, 3])
        ctxT = sb("ctxT", [P, B * SK])
        maskT = sb("maskT", [SK, S], U8)
        maskneg = sb("maskneg", [SK, S], BF16)
        neghalf = sb("neghalf", [P, QT])
        xTv = sb("xTv", [P, S])
        xT = sb("xT", [P, S])
        xres = sb("xres", [P, NT, P])
        x1 = sb("x1", [P, QT, P])
        x2 = sb("x2", [P, QT, P])
        x2T = sb("x2T", [P, B * S])
        x2Th = sb("x2Th", [P, B * S], F32R)
        x2Tl = sb("x2Tl", [P, B * S], F32R)
        qk32 = sb("qk32", [P, 2 * S])
        qkparts = sb("qkparts", [P, 2, 3, S], BF16)
        qkrest = sb("qkrest", [P, 2 * S])
        q2_32 = sb("q2_32", [P, S])
        q2parts = sb("q2parts", [P, 3, S], BF16)
        q2rest = sb("q2rest", [P, S])
        qS = sb("qS", [K1M, 2, H1, S], BF16)
        kS = sb("kS", [K1M, 2, H1, S], BF16)
        q2S = sb("q2S", [K2M, H2, S], BF16)
        k2S = sb("k2S", [K2M, H2, B * SK], BF16)
        k2cur = sb("k2cur", [K2M, H2, SK], BF16)
        vaug = sb("vaug", [P, QT, H1, 32])
        v2aug = sb("v2aug", [P, B, PAIRS, 32])
        v2cur = sb("v2cur", [P, PAIRS, 32])
        probs1 = sb("probs1", [P, H1, 2 * S])
        probs2 = sb("probs2", [P, 4, 2 * S])
        k2_32 = sb("k2_32", [P, B * SK])
        k2rest = sb("k2rest", [P, B * SK])
        k2parts = sb("k2parts", [P, 3, B * SK], BF16)
        bdV, bdU = (probs2[:].rearrange("p a q -> p (a q)")[:, i * 6 * P:(i + 1) * 6 * P]
                    .rearrange("p (i c d) -> p i c d", i=3, c=2) for i in range(2))
        mx1 = sb("mx1", [P, QT, H1])
        mx2 = sb("mx2", [P, QT, H2])
        mneg1 = sb("mneg1", [P, QT, 2 * H1], BF16)
        mneg2 = sb("mneg2", [P, QT, 2 * H2], BF16)
        mrow1 = sb("mrow1", [2 * H1, S], BF16)
        mrow2 = sb("mrow2", [2 * H2, S], BF16)
        o1s = sb("o1s", [P, 2, S])
        o2s = sb("o2s", [P, 2, S])
        rsum1 = sb("rsum1", [P, QT * H1])
        rsum2 = sb("rsum2", [P, QT * H2])
        att1 = sb("att1", [P, QT * H1, DH1])
        att2 = sb("att2", [P, QT * H2, DH2])
        att2T = sb("att2T", [P, S])
        y1 = sb("y1", [P, QT, P])
        y2 = sb("y2", [P, QT, P])
        st1 = sb("st1", [P, QT, 6])
        st2 = sb("st2", [P, QT, 6])
        mv1 = sb("mv1", [P, QT, 2])
        mv2 = sb("mv2", [P, QT, 2])
        ve1 = sb("ve1", [P, QT])
        ve2 = sb("ve2", [P, QT])
        rs1 = sb("rs1", [P, QT])
        rs2 = sb("rs2", [P, QT])
        x1Ts = sb("x1Ts", [P, S])
        w13 = sb("w13", [P, 3, 2, HF])
        w13h = sb("w13h", [P, NE, 2, HF], F32R)
        w13l = sb("w13l", [P, NE, 2, HF], F32R)
        w2 = sb("w2", [P, NE, CH, P])
        rwT = sb("rwT", [P, E])
        ebB = sb("ebB", [P, E])
        iotaE = sb("iotaE", [P, E])
        logits = sb("logits", [P, NT, E])
        top = sb("top", [P, NT, 8])
        topi = sb("topi", [P, NT, 8], U32)
        topf = sb("topf", [P, NT, 2])
        gap = sb("gap", [P, NT])
        rw = sb("rw", [P, NT, 2])
        den = sb("den", [P, NT])
        pick = sb("pick", [P, NT, E])
        cw = sb("cw", [P, NT, NE])
        hid, silu = probs1[:, 0:2 * CH, :], probs1[:, 2 * CH:2 * CH + 2, :]
        acc = xres
        yout = probs2[:].rearrange("p a (m d) -> p (a m) d", d=P)
        st3 = sb("st3", [P, GQ, 6])
        mv3 = sb("mv3", [P, GQ, 2])
        ve3 = sb("ve3", [P, GQ])
        rs3 = sb("rs3", [P, GQ])
        nh3 = sb("nh3", [P, GQ])

        ps_max = [pb(f"ps_max{i}", [P, 512]) for i in range(2)]
        ps_exp = [pb(f"ps_exp{i}", [P, 512]) for i in range(3)]
        ps_pv = pb("ps_pv", [P, 512])
        ps_in = pb("ps_in", [P, 512])
        ps_post = pb("ps_post", [P, 512])

        dram_qk = nc.dram_tensor("qk_parts", [B, 2, 3, P, S], BF16).ap()
        dram_q2 = nc.dram_tensor("q2_parts", [B, 3, P, S], BF16).ap()
        dram_k2 = nc.dram_tensor("k2_parts", [3, P, B * SK], BF16).ap()

        names = """loaded_low loaded_bqk loaded_ident w_split x2T_split loaded_wx loaded_x loaded_xv loaded_res loaded_ffn loaded_shared loaded_router w_high
            consts_set ones_set bd_built w_ready w_kept k2_ready k2_kept k2_split k2_out k2_stacked v2_ready v2_kept
            mask_set rows_set rows_loaded res_set
            qk_ready qk_kept qk_split qk_out qk_stacked v_ready v_kept
            max_ready max_done m_split mT_ready mT_kept m_stacked
            sc_ready exp_done pv1_done o1_kept o1T_ready ln1 rstd1 res1 k2cur_set v2cur_set acc_set x1T_ready x1T_kept
            q2_ready q2_kept q2_split q2_out q2_stacked
            xmax_ready xmax_done m2_split m2T_ready m2T_kept m2_stacked
            xsc_ready xexp_done pv2_done o2_kept o2T_ready ln2 att2T_ready att2T_kept wo_ready rstd2
            x2T_ready x2T_kept
            lg_ready route gap_exp up_ready silu_done hid_done down_ready acc_done ln3 rstd3 stored carrier""".split()
        s = {n: sem(n) for n in names}

        block = ctx.enter_context(nc.Block())

        class Steps:
            def __init__(self, eng, name, base=0):
                self.eng, self.sem, self.base, self.k = eng, s[name], base, 0

            def inc(self, ins):
                ins.then_inc(self.sem, 1)
                self.k += 1

            def wait(self):
                wait_alone(self.eng, self.sem, self.base + self.k, s["carrier"])

            def then(self, ins):
                self.inc(ins)
                self.wait()

        def tiles_of(buf, b):
            return buf[:, bass.ds(b * QT, QT), :]

        def tokens_of(buf, b, n=S):
            return buf[:, bass.ds(b * n, n)]

        @block.sync
        def _(sp):
            def load(dst, src, name):
                sp.dma_start(dst, src).then_inc(s[name], 16)

            load(lowV[:], t["lowV"], "loaded_low")
            load(lowU[:], t["lowU"], "loaded_low")
            load(headmask[:], t["headmask"], "loaded_low")
            load(bqk[:], t["bqk"], "loaded_bqk")
            load(xT[:], t["xT"][:, 0:S], "loaded_x")
            load(ident[:], t["ident"], "loaded_ident")
            load(maskT[:], t["maskT"], "loaded_ident")
            load(wx[:], t["wx"], "loaded_wx")
            load(bx[:], t["bx"], "loaded_wx")
            load(ctxT[:], t["ctxT"], "loaded_wx")
            load(xres[:], t["x"].rearrange("(n p) d -> p n d", p=P), "loaded_res")
            load(bvB[:], t["bv1"].partition_broadcast(P), "loaded_res")
            load(boB[:], t["bo"].partition_broadcast(P), "loaded_res")

            load(kS[M1:K1M, :, :, :].rearrange("p a h t -> p (a h t)").bitcast(F32), t["onesrow"][:, 0:H1 * S],
                 "rows_loaded")
            load(k2S[K2:K2M, :, :].rearrange("p h t -> p (h t)").bitcast(F32), t["onesrow"], "rows_loaded")

            def stack_q(rows, parts, dh, name):
                at = 0
                for a, n in enumerate(TERMS):
                    src = parts[a].rearrange("(d h) t -> d (h t)", d=dh)
                    load(rows(at * dh, n * dh), src.unsqueeze(0).to_broadcast([n, dh, src.shape[1]]), name)
                    at += n

            def stack_k(rows, parts, dh, name):
                at = 0
                for n in TERMS:
                    load(rows(at * dh, n * dh), parts[0:n].rearrange("a (d h) t -> (a d) (h t)", d=dh), name)
                    at += n

            def rows_of(buf, first=0):
                return lambda at, n: buf[first + at:first + at + n].rearrange("p h t -> p (h t)")

            def step(b):
                b0, b1, b2, b3, b4 = b
                if on(b3):
                    wait_alone(sp, s["q2_out"], 16 * (b3 + 1), s["carrier"])
                    if on(b4):
                        wait_alone(sp, s["xsc_ready"], 4 * (b4 + 1), s["carrier"])
                    stack_q(rows_of(q2S, C2), dram_q2[b3], DH2, "q2_stacked")
                if on(b0):
                    wait_alone(sp, s["qk_ready"], b0 + 1, s["carrier"])
                    load(xT[:], t["xT"][:, bass.ds((b0 + 1) % B * S, S)], "loaded_x")
                if on(b0):
                    wait_alone(sp, s["qk_split"], SPLIT_STEPS * (b0 + 1), s["carrier"])
                    load(dram_qk[b0].rearrange("j a p t -> p (j a) t"),
                         qkparts[:].rearrange("p j a t -> p (j a) t"), "qk_out")
                if on(b1):
                    wait_alone(sp, s["mT_kept"], b1 + 1, s["carrier"])
                    load(qS[M1:M1 + 2, b1 % 2, :, :].rearrange("p h t -> p (h t)"), mrow1[:], "m_stacked")
                if on(b0):
                    wait_alone(sp, s["qk_out"], 16 * (b0 + 1), s["carrier"])
                    if not isinstance(b0, int) or b0 >= 2:
                        wait_alone(sp, s["sc_ready"], H1 * (b0 - 1), s["carrier"])
                    stack_q(rows_of(qS[:, b0 % 2]), dram_qk[b0, 0], DH1, "qk_stacked")
                    stack_k(rows_of(kS[:, b0 % 2]), dram_qk[b0, 1], DH1, "qk_stacked")
                if on(b0):
                    if on(b1):
                        wait_alone(sp, s["v_ready"], b1 + 1, s["carrier"])
                    load(xTv[:], t["xT"][:, bass.ds(b0 * S, S)], "loaded_xv")
                if on(b3):
                    wait_alone(sp, s["m2T_kept"], b3 + 1, s["carrier"])
                    load(q2S[K2:K2 + 2, :, :].rearrange("p h t -> p (h t)"), mrow2[:], "m2_stacked")
                if on(b2):
                    wait_alone(sp, s["q2_split"], SPLIT_STEPS * (b2 + 1), s["carrier"])
                    load(dram_q2[b2].rearrange("a p t -> p a t"), q2parts[:], "q2_out")
                if isinstance(b0, int) and b0 == 1:
                    sp.wait_ge(s["k2_split"], SPLIT_STEPS)
                    load(dram_k2.rearrange("a p t -> p a t"), k2parts[:], "k2_out")
                    sp.wait_ge(s["k2_out"], 16)
                    stack_k(rows_of(k2S, C2), dram_k2, DH2, "k2_stacked")

            pipeline(sp, step)
            outv = t["out"].rearrange("(n p) d -> p n d", p=P)
            with sp.Fori(0, NG) as g:
                wait_alone(sp, s["ln3"], LN3_STEPS * (g + 1), s["carrier"])
                load(outv[:, bass.ds(g * GQ, GQ), :], yout[:, bass.ds(g * GQ, GQ), :], "stored")
            sp.wait_ge(s["stored"], 16 * NG)

        @block.gpsimd
        def _(pool):
            g = nc.gpsimd
            g.memset(vaug[:], 0.0).then_inc(s["rows_set"], 1)
            g.memset(v2aug[:], 0.0).then_inc(s["rows_set"], 1)
            pool.wait_ge(s["rows_set"], 2)
            g.memset(vaug[:, :, :, DH1:DH1 + 1], 1.0).then_inc(s["rows_set"], 1)
            g.memset(neghalf[:], -0.5).then_inc(s["rows_set"], 1)
            g.memset(nh3[:], -0.5).then_inc(s["rows_set"], 1)
            g.memset(cw[:, :, E:NE], 1.0).then_inc(s["rows_set"], 1)

            def load_expert(e, slot, w13_src, w2_src, name):
                pool.dma_start(w13[:, slot], w13_src).then_inc(s[name], 16)
                pool.dma_start(w2[:, e], w2_src).then_inc(s[name], 16)

            def split_expert(e, slot, k):
                wait_alone(pool, s["w_high"], k + 1, s["carrier"])
                g.tensor_tensor(w13l[:, e], w13[:, slot], w13h[:, e], ALU.subtract).then_inc(s["w_split"], 1)

            pool.dma_start(rwT[:], t["rwT"]).then_inc(s["loaded_router"], 16)
            pool.dma_start(ebB[:], t["ebias"].partition_broadcast(P)).then_inc(s["loaded_router"], 16)
            pool.dma_start(iotaE[:], t["iotaE"]).then_inc(s["loaded_router"], 16)

            def split(st, src, hi, mid, lo, rest):
                st.inc(g.tensor_tensor(mid, src, hi, ALU.subtract))
                st.then(g.tensor_tensor(rest, src, hi, ALU.subtract))
                st.then(g.tensor_tensor(lo, rest, mid, ALU.subtract))

            def split_k2():
                pool.wait_ge(s["k2_kept"], 2)
                split(Steps(pool, "k2_split"), k2_32[:], *(k2parts[:, a, :] for a in range(3)), k2rest[:])

            def add_value_bias():
                pool.wait_ge(s["loaded_res"], 48)
                g.tensor_tensor(xres[:], xres[:], bvB[:].unsqueeze(1).to_broadcast([P, NT, P]),
                                ALU.add).then_inc(s["res_set"], 1)

            def rstd(ln, name, b, mv, ve, rs):
                wait_alone(pool, s[ln], LN_STEPS * b + LN_STATS, s["carrier"])
                st = Steps(pool, name, 2 * b)
                st.then(g.tensor_scalar(ve[:], mv[:, :, 1], EPS, None, ALU.add))
                st.inc(g.tensor_tensor(rs[:], ve[:], neghalf[:], ALU.pow))

            def step(b):
                b0, b1, b2, b3, b4 = b
                if on(b0):
                    wait_alone(pool, s["qk_kept"], b0 + 1, s["carrier"])
                    wait_alone(pool, s["qk_out"], 16 * b0, s["carrier"])
                    split(Steps(pool, "qk_split", SPLIT_STEPS * b0), qk32[:].rearrange("p (j t) -> p j t", j=2),
                          *(qkparts[:, :, a, :] for a in range(3)), qkrest[:].rearrange("p (j t) -> p j t", j=2))
                    if isinstance(b0, int) and b0 == 0:
                        split_k2()
                    if isinstance(b0, int) and b0 == 1:
                        add_value_bias()
                        load_expert(E, 2, t["sw13"][:, 0], t["sw2"][:, 0], "loaded_shared")
                    if not isinstance(b0, int) or b0 >= 1:
                        wait_alone(pool, s["loaded_ffn"], 32 * b0, s["carrier"])
                    load_expert(b0, b0 % 2, t["w13"][:, b0], t["w2"][:, b0], "loaded_ffn")
                if on(b2):
                    rstd("ln1", "rstd1", b2, mv1, ve1, rs1)
                if on(b4):
                    rstd("ln2", "rstd2", b4, mv2, ve2, rs2)
                if on(b2):
                    wait_alone(pool, s["ln1"], LN_STEPS * (b2 + 1), s["carrier"])
                    g.tensor_tensor(tiles_of(xres, b2), x1[:],
                                    boB[:].unsqueeze(1).to_broadcast([P, QT, P]), ALU.add).then_inc(s["res1"], 1)
                    wait_alone(pool, s["q2_kept"], 2 * (b2 + 1), s["carrier"])
                    wait_alone(pool, s["q2_out"], 16 * b2, s["carrier"])
                    split(Steps(pool, "q2_split", SPLIT_STEPS * b2), q2_32[:], *(q2parts[:, a, :] for a in range(3)),
                          q2rest[:])
                if on(b4):
                    wait_alone(pool, s["ln2"], LN_STEPS * (b4 + 1), s["carrier"])
                    g.tensor_copy(tiles_of(acc, b4), x2[:]).then_inc(s["acc_set"], 1)
                if on(b1):
                    split_expert(b1, b1 % 2, b1)
                elif isinstance(b2, int) and b2 == B - 1:
                    split_expert(E, 2, E)
                if on(b4):
                    wait_alone(pool, s["x2T_kept"], 2 * (b4 + 1), s["carrier"])
                    g.tensor_tensor(tokens_of(x2Tl, b4), tokens_of(x2T, b4), tokens_of(x2Th, b4),
                                    ALU.subtract).then_inc(s["x2T_split"], 1)

            pipeline(pool, step)
            with pool.Fori(0, NG) as i:
                wait_alone(pool, s["ln3"], LN3_STEPS * i + 2 * GQ, s["carrier"])
                st = Steps(pool, "rstd3", 2 * i)
                st.then(g.tensor_scalar(ve3[:], mv3[:, :, 1], EPS, None, ALU.add))
                st.inc(g.tensor_tensor(rs3[:], ve3[:], nh3[:], ALU.pow))

        @block.tensor
        def _(pe):
            mm = nc.tensor.matmul
            tr = nc.tensor.transpose
            pe.wait_ge(s["bd_built"], 12)
            for i in range(3):
                for c in range(2):
                    m = mm(ps_in[:, i * P:(i + 1) * P], bdV[:, i, c, :], bdU[:, i, c, :], start=c == 0, stop=c == 1)
            m.then_inc(s["w_ready"], 1)
            pe.wait_ge(s["w_kept"], 1)

            def context():
                pe.wait_ge(s["loaded_wx"], 48)
                mm(ps_post[:], wx[:, 1, :], ctxT[:], start=True, stop=True).then_inc(s["k2_ready"], 1)
                for b in range(B):
                    for a in range(2):
                        m = mm(ps_exp[b // 4][64 * a:64 * a + 64, (b % 4) * P:(b % 4 + 1) * P],
                               ctxT[:, b * SK:(b + 1) * SK], wx[:, 2, :], start=True, stop=True,
                               tile_position=(0, 64 * a))
                m.then_inc(s["v2_ready"], 1)

            def max_tile(b, i):
                if i >= 2:
                    pe.wait_ge(s["max_done"], H1 * b + i - 1)
                qt, hp = divmod(i, H1 // 2)
                for j in range(2):
                    h = 2 * hp + j
                    m = mm(ps_max[i % 2][:, j * S:(j + 1) * S], qS[0:K1, b % 2, h, qt * P:(qt + 1) * P],
                           kS[0:K1, b % 2, h, :], start=True, stop=True)
                m.then_inc(s["max_ready"], 1)

            def score_tile(b, h):
                if h >= 3:
                    pe.wait_ge(s["exp_done"], H1 * b + h - 2)
                for kt in range(QT):
                    m = mm(ps_exp[(4 + h) % 3][:, kt * S:(kt + 1) * S], kS[:, b % 2, h, kt * P:(kt + 1) * P],
                           qS[:, b % 2, h, :], start=True, stop=True)
                m.then_inc(s["sc_ready"], 1)

            def pv_group(b, g):
                pe.wait_ge(s["exp_done"], H1 * b + 4 * g + 4)
                for kt in range(QT):
                    for j in range(4):
                        h = 4 * g + j
                        m = mm(ps_pv[32 * j:32 * j + 32, g * S:(g + 1) * S], vaug[:, kt, h, :],
                               probs1[:, h, kt * S:(kt + 1) * S], start=kt == 0, stop=kt == QT - 1,
                               tile_position=(0, 32 * j))
                m.then_inc(s["pv1_done"], 1)

            def xscore_tile(b, i):
                if i == 0:
                    pe.wait_ge(s["k2cur_set"], b + 1)
                if i == 3:
                    pe.wait_ge(s["xexp_done"], 4 * b + 1)
                for pr in range(2):
                    for a in range(2):
                        h = 4 * i + 2 * pr + a
                        m = mm(ps_exp[i % 3][64 * a:64 * a + 64, pr * S:(pr + 1) * S],
                               k2cur[:, h, :], q2S[:, h, :], start=True, stop=True,
                               tile_position=(0, 64 * a))
                m.then_inc(s["xsc_ready"], 1)

            def xpv_group(b, g):
                pe.wait_ge(s["v2cur_set"], b + 1)
                pe.wait_ge(s["xexp_done"], 4 * b + 2 * g + 2)
                for j in range(4):
                    pr = 4 * g + j
                    m = mm(ps_pv[32 * j:32 * j + 32, g * S:(g + 1) * S], v2cur[:, pr, :],
                           probs2[:, pr // 2, (pr % 2) * S:(pr % 2 + 1) * S], start=True, stop=True,
                           tile_position=(0, 32 * j))
                m.then_inc(s["pv2_done"], 1)

            def xmax_tile(b, i):
                if i >= 2:
                    pe.wait_ge(s["xmax_done"], 4 * b + i - 1)
                qt, hh = divmod(i, 2)
                for j in range(8):
                    h = 8 * hh + j
                    m = mm(ps_max[(i + 1) % 2][:, j * SK:(j + 1) * SK], q2S[0:K2, h, qt * P:(qt + 1) * P],
                           k2S[0:K2, h, bass.ds(b * SK, SK)], start=True, stop=True)
                m.then_inc(s["xmax_ready"], 1)

            def transpose_heads(b, src, name):
                for qt in range(QT):
                    for g in range(2):
                        c = (qt * 2 + g) * P
                        m = tr(ps_post[:, c:c + P], src[:, g, qt * P:(qt + 1) * P], ident[:])
                m.then_inc(s[name], 1)

            def router(n0, n1):
                for n in range(n0, n1):
                    m = mm(ps_in[:, n * E:(n + 1) * E], x2T[:, n * P:(n + 1) * P], rwT[:], start=True, stop=True)
                m.then_inc(s["lg_ready"], 1)

            def transpose_tiles(src, name):
                for qt in range(QT):
                    m = tr(ps_post[:, qt * P:(qt + 1) * P], src(qt), ident[:])
                m.then_inc(s[name], 1)

            def transpose_max(mneg, n, name):
                for qt in range(QT):
                    m = tr(ps_max[0].bitcast(BF16)[0:n, qt * P:(qt + 1) * P], mneg[:, qt, :], identb[:])
                m.then_inc(s[name], 1)

            def step(b):
                b0, b1, b2, b3, b4 = b
                if on(b0):
                    if on(b1) and (not isinstance(b1, int) or b1 >= 1):
                        pe.wait_ge(s["v_kept"], b1)
                    elif on(b1):
                        pe.wait_ge(s["qk_kept"], 1)
                    pe.wait_ge(s["loaded_x"], 16 * (b0 + 1))
                    for i in range(2):
                        m = mm(ps_in[:, i * S:(i + 1) * S], wqkv[:, i, :], xT[:], start=True, stop=True)
                    m.then_inc(s["qk_ready"], 1)
                    if isinstance(b0, int) and b0 == 0:
                        context()
                if on(b1):
                    pe.wait_ge(s["qk_stacked"], 16 * 6 * (b1 + 1))
                    if on(b3) and (not isinstance(b3, int) or b3 >= 1):
                        pe.wait_ge(s["m2T_kept"], b3)
                    max_tile(b1, 0)
                    max_tile(b1, 1)
                if on(b2):
                    pv_group(b2, 1)
                if on(b4):
                    pe.wait_ge(s["m2_stacked"], 16 * (b4 + 1))
                for i in range(2):
                    if on(b4):
                        xscore_tile(b4, i)
                    if on(b1):
                        max_tile(b1, i + 2)
                if on(b2):
                    pe.wait_ge(s["o1_kept"], b2 + 1)
                    if not isinstance(b2, int) or b2 >= 1:
                        pe.wait_ge(s["q2_kept"], 2 * b2)
                    if on(b4):
                        pe.wait_ge(s["x2T_kept"], 2 * b4)
                    transpose_heads(b2, o1s, "o1T_ready")
                if on(b4):
                    xscore_tile(b4, 2)
                if on(b1):
                    max_tile(b1, 4)
                if on(b4):
                    xscore_tile(b4, 3)
                if on(b1):
                    max_tile(b1, 5)
                if on(b4):
                    xpv_group(b4, 0)
                if on(b1):
                    max_tile(b1, 6)
                if on(b4):
                    xpv_group(b4, 1)
                if last_step(b4):
                    pe.wait_ge(s["loaded_router"], 48)
                    router(0, 5)
                if on(b1):
                    max_tile(b1, 7)
                    if on(b0):
                        pe.wait_ge(s["qk_kept"], b0 + 1)
                    pe.wait_ge(s["loaded_xv"], 16 * (b1 + 1))
                    for qt in range(QT):
                        m = mm(ps_in[:, qt * P:(qt + 1) * P], xTv[:, qt * P:(qt + 1) * P], wqkv[:, 2, :],
                               start=True, stop=True)
                    m.then_inc(s["v_ready"], 1)
                if on(b4):
                    pe.wait_ge(s["o2_kept"], b4 + 1)
                    if on(b2):
                        pe.wait_ge(s["ln1"], LN_STEPS * b2 + 2)
                    else:
                        pe.wait_ge(s["x2T_kept"], 2 * b4)
                    transpose_heads(b4, o2s, "o2T_ready")
                if last_step(b4):
                    router(5, 10)
                if on(b1):
                    pe.wait_ge(s["m_split"], 2 * (b1 + 1))
                    transpose_max(mneg1, 2 * H1, "mT_ready")
                if on(b3):
                    pe.wait_ge(s["q2_stacked"], 16 * 3 * (b3 + 1))
                    if isinstance(b3, int) and b3 == 0:
                        pe.wait_ge(s["mask_set"], 2)
                        pe.wait_ge(s["k2_stacked"], 16 * 3)
                        pe.wait_ge(s["rows_loaded"], 32)
                    xmax_tile(b3, 0)
                if on(b4):
                    pe.wait_ge(s["ln2"], LN_STEPS * b4 + 2)
                    transpose_tiles(lambda qt: att2[:, qt * H2:(qt + 1) * H2, :].rearrange("p h d -> p (h d)"),
                                    "att2T_ready")
                if last_step(b4):
                    router(10, NT - QT)
                if on(b3):
                    if on(b1):
                        pe.wait_ge(s["mT_kept"], b1 + 1)
                    xmax_tile(b3, 1)
                if on(b4):
                    pe.wait_ge(s["att2T_kept"], b4 + 1)
                    for qt in range(QT):
                        m = mm(ps_post[:, S + qt * P:S + (qt + 1) * P], att2T[:, qt * P:(qt + 1) * P], wx[:, 3, :],
                               start=True, stop=True)
                    m.then_inc(s["wo_ready"], 1)
                if on(b1):
                    pe.wait_ge(s["m_stacked"], 16 * (b1 + 1))
                    if isinstance(b1, int) and b1 == 0:
                        pe.wait_ge(s["rows_loaded"], 32)
                        pe.wait_ge(s["v2_kept"], 4)
                    score_tile(b1, 0)
                    score_tile(b1, 1)
                if on(b3):
                    xmax_tile(b3, 2)
                if on(b1):
                    score_tile(b1, 2)
                    score_tile(b1, 3)
                if on(b3):
                    xmax_tile(b3, 3)
                if on(b2):
                    if on(b4):
                        pe.wait_ge(s["ln2"], LN_STEPS * b4 + 3)
                    pe.wait_ge(s["ln1"], LN_STEPS * (b2 + 1))
                    transpose_tiles(lambda qt: x1[:, qt, :], "x1T_ready")
                if on(b1):
                    score_tile(b1, 4)
                    score_tile(b1, 5)
                if on(b2):
                    pe.wait_ge(s["x1T_kept"], b2 + 1)
                    mm(ps_post[:, S:2 * S], wx[:, 0, :], x1Ts[:], start=True, stop=True).then_inc(s["q2_ready"], 1)
                if on(b1):
                    pe.wait_ge(s["v_kept"], b1 + 1)
                    if isinstance(b1, int) and b1 == 0:
                        pe.wait_ge(s["rows_set"], 3)
                    if on(b4):
                        pe.wait_ge(s["o2_kept"], b4 + 1)
                    pv_group(b1, 0)
                if on(b3):
                    pe.wait_ge(s["m2_split"], 2 * (b3 + 1))
                    transpose_max(mneg2, 2 * H2, "m2T_ready")
                if on(b1):
                    score_tile(b1, 6)
                    score_tile(b1, 7)
                if on(b4):
                    if on(b2):
                        pe.wait_ge(s["q2_kept"], 2 * (b2 + 1))
                    pe.wait_ge(s["ln2"], LN_STEPS * (b4 + 1))
                    transpose_tiles(lambda qt: x2[:, qt, :], "x2T_ready")

            pipeline(pe, step)

            pe.wait_ge(s["x2T_kept"], 2 * B)
            pe.wait_ge(s["route"], 1)
            router(NT - QT, NT)

            up = [(ps_exp[0], ps_exp[1]), (ps_exp[2], ps_pv)]
            down = [ps_max[0], ps_max[1]]

            def up_unit(g, u):
                gate, lin = up[u % 2]
                if not (isinstance(g, int) and u < 2):
                    pe.wait_ge(s["hid_done"], g * NE * CH + u - 1)
                e, c = divmod(u, CH)
                xh, xl = x2Th[:, bass.ds(g * GT, GT)], x2Tl[:, bass.ds(g * GT, GT)]
                for i, out in ((0, gate), (1, lin)):
                    for j, (w, x) in enumerate(((w13l, xh), (w13h, xl), (w13h, xh))):
                        m = mm(out[:], w[:, e, i, c * P:(c + 1) * P], x, start=j == 0, stop=j == 2)
                m.then_inc(s["up_ready"], 1)

            def down_unit(g, e):
                n = g * NE + e
                pe.wait_ge(s["hid_done"], (n + 1) * CH)
                if not (isinstance(g, int) and e < 2):
                    pe.wait_ge(s["acc_done"], n - 1)
                for q in range(GT // P):
                    for c in range(CH):
                        m = mm(down[e % 2][:, q * P:(q + 1) * P], hid[:, (e % 2) * CH + c, q * P:(q + 1) * P],
                               w2[:, e, c, :], start=c == 0, stop=c == CH - 1)
                m.then_inc(s["down_ready"], 1)

            def group(g):
                for e in range(NE):
                    for c in range(CH):
                        up_unit(g, e * CH + c)
                    if e >= 1:
                        down_unit(g, e - 1)
                down_unit(g, NE - 1)

            pe.wait_ge(s["loaded_ffn"], 32 * E)
            pe.wait_ge(s["loaded_shared"], 32)
            pe.wait_ge(s["w_split"], NE)
            pe.wait_ge(s["x2T_split"], B)
            group(0)
            with pe.Fori(1, NG) as g:
                group(g)

        @block.scalar
        def _(act):
            a = nc.scalar.activation

            def copy(out, in_, name, bias=None):
                if bias is None:
                    a(out, in_, ACT.Copy).then_inc(s[name], 1)
                else:
                    a(out, in_, ACT.Identity, bias=bias).then_inc(s[name], 1)

            act.wait_ge(s["w_ready"], 1)
            copy(wqkv[:].rearrange("p i d -> p (i d)"), ps_in[:, 0:3 * P], "w_kept")

            def high_part(e, slot, k):
                if isinstance(k, int) and k == E:
                    act.wait_ge(s["loaded_shared"], 32)
                else:
                    act.wait_ge(s["loaded_ffn"], 32 * (k + 1))
                copy(w13h[:, e], w13[:, slot], "w_high")

            def exp1(b, h):
                act.wait_ge(s["sc_ready"], H1 * b + h + 1)
                a(probs1[:, h, :], ps_exp[(4 + h) % 3][:], ACT.Exp, scale=SCALE1).then_inc(s["exp_done"], 1)

            def step(b):
                b0, b1, b2, b3, b4 = b
                if on(b0):
                    act.wait_ge(s["qk_ready"], b0 + 1)
                    act.wait_ge(s["qk_split"], SPLIT_STEPS * b0)
                    act.wait_ge(s["qk_out"], 16 * b0)
                    for j in range(2):
                        a(qk32[:, j * S:(j + 1) * S], ps_in[:, j * S:(j + 1) * S], ACT.Identity, bias=bqk[:, j:j + 1])
                        m = a(qkparts[:, j, 0, :], ps_in[:, j * S:(j + 1) * S], ACT.Identity, bias=bqk[:, j:j + 1])
                    m.then_inc(s["qk_kept"], 1)
                    if isinstance(b0, int) and b0 == 0:
                        act.wait_ge(s["k2_ready"], 1)
                        copy(k2_32[:], ps_post[:], "k2_kept", bx[:, 1:2])
                        copy(k2parts[:, 0, :], ps_post[:], "k2_kept", bx[:, 1:2])
                if on(b2):
                    act.wait_ge(s["pv1_done"], 2 * (b2 + 1))
                    copy(o1s[:].rearrange("p g q -> p (g q)"), ps_pv[:], "o1_kept")
                if on(b4):
                    for i in range(4):
                        act.wait_ge(s["xsc_ready"], 4 * b4 + i + 1)
                        a(probs2[:, i, :], ps_exp[i % 3][:], ACT.Exp, scale=SCALE2).then_inc(s["xexp_done"], 1)
                if on(b4):
                    act.wait_ge(s["pv2_done"], 2 * (b4 + 1))
                    copy(o2s[:].rearrange("p g q -> p (g q)"), ps_pv[:], "o2_kept")
                if on(b1):
                    act.wait_ge(s["mT_ready"], b1 + 1)
                    act.wait_ge(s["m_stacked"], 16 * b1)
                    copy(mrow1[:], ps_max[0].bitcast(BF16)[0:2 * H1, 0:S], "mT_kept")
                if on(b4):
                    act.wait_ge(s["att2T_ready"], b4 + 1)
                    copy(att2T[:], ps_post[:, 0:S], "att2T_kept", bx[:, 2:3])
                if on(b1):
                    for h in range(4):
                        exp1(b1, h)
                if on(b2):
                    act.wait_ge(s["x1T_ready"], b2 + 1)
                    copy(x1Ts[:], ps_post[:, 0:S], "x1T_kept")
                if on(b1):
                    exp1(b1, 4)
                    exp1(b1, 5)
                if on(b2):
                    act.wait_ge(s["q2_ready"], b2 + 1)
                    act.wait_ge(s["q2_split"], SPLIT_STEPS * b2)
                    act.wait_ge(s["q2_out"], 16 * b2)
                    copy(q2_32[:], ps_post[:, S:2 * S], "q2_kept", bx[:, 0:1])
                    copy(q2parts[:, 0, :], ps_post[:, S:2 * S], "q2_kept", bx[:, 0:1])
                if on(b3):
                    act.wait_ge(s["m2T_ready"], b3 + 1)
                    act.wait_ge(s["m2_stacked"], 16 * b3)
                    copy(mrow2[:], ps_max[0].bitcast(BF16)[0:2 * H2, 0:S], "m2T_kept")
                if on(b1):
                    exp1(b1, 6)
                    exp1(b1, 7)
                if on(b4):
                    act.wait_ge(s["x2T_ready"], b4 + 1)
                    copy(tokens_of(x2T, b4), ps_post[:, 0:S], "x2T_kept")
                    copy(tokens_of(x2Th, b4), ps_post[:, 0:S], "x2T_kept")
                if on(b1):
                    high_part(b1, b1 % 2, b1)
                elif isinstance(b2, int) and b2 == B - 1:
                    high_part(E, 2, E)

            pipeline(act, step)
            act.wait_ge(s["route"], ROUTE_GAP)
            a(rw[:, :, 1], gap[:], ACT.Exp).then_inc(s["gap_exp"], 1)

            gates = [ps_exp[0], ps_exp[2]]

            def silus(g):
                for u in range(NE * CH):
                    act.wait_ge(s["up_ready"], g * NE * CH + u + 1)
                    if not (isinstance(g, int) and u < 2):
                        act.wait_ge(s["hid_done"], g * NE * CH + u - 1)
                    a(silu[:, u % 2, :], gates[u % 2][:], ACT.Silu).then_inc(s["silu_done"], 1)

            silus(0)
            with act.Fori(1, NG) as g:
                silus(g)

        @block.vector
        def _(dve):
            v = nc.vector
            dve.wait_ge(s["loaded_low"], 48)
            for i in range(3):
                for c in range(2):
                    mask = headmask[:, c, :].unsqueeze(2).to_broadcast([P, H1, DH1])
                    for dst, src in ((bdV, lowV), (bdU, lowU)):
                        order = "p (d h) -> p h d" if dst is bdU and i < 2 else "p (h d) -> p h d"
                        v.tensor_tensor(dst[:, i, c, :].rearrange(order, h=H1),
                                        src[:, i, c, :].unsqueeze(1).to_broadcast([P, H1, DH1]), mask,
                                        ALU.mult).then_inc(s["bd_built"], 1)
            dve.wait_ge(s["loaded_ident"], 32)
            v.tensor_copy(identb[:], ident[:]).then_inc(s["consts_set"], 1)
            v.tensor_scalar(maskneg[:], maskT[:], 0.0, MASKED, ALU.is_equal, ALU.mult).then_inc(s["consts_set"], 1)
            dve.wait_ge(s["consts_set"], 2)
            v.tensor_copy(q2S[0:SK, :, :], maskneg[:].unsqueeze(1).to_broadcast([SK, H2, S]))\
                .then_inc(s["mask_set"], 1)
            v.tensor_copy(k2S[0:SK, :, :].rearrange("p h (b k) -> p (h b) k", b=B),
                          identb[0:SK, 0:SK].unsqueeze(1).to_broadcast([SK, H2 * B, SK])).then_inc(s["mask_set"], 1)
            dve.wait_ge(s["rows_set"], 2)
            v.memset(v2aug[0:64, :, :, DH2:DH2 + 1], 1.0).then_inc(s["ones_set"], 1)
            v.memset(v2aug[64:P, :, :, 16 + DH2:17 + DH2], 1.0).then_inc(s["ones_set"], 1)
            dve.wait_ge(s["v2_ready"], 1)
            for half in range(2):
                for a in range(2):
                    src = ps_exp[half][64 * a:64 * a + 64, :].rearrange("p (n a d) -> p n a d", a=2, d=DH2)
                    dst = v2aug[64 * a:64 * a + 64, 4 * half:4 * half + 4, :, 16 * a:16 * a + DH2]
                    v.tensor_copy(dst.rearrange("p b r d -> p (b r) d"), src[:, :, a, :]).then_inc(s["v2_kept"], 1)

            def max_tile(b, i):
                dve.wait_ge(s["max_ready"], H1 * b + i + 1)
                qt, hp = divmod(i, H1 // 2)
                v.tensor_reduce(mx1[:, qt, 2 * hp:2 * hp + 2], ps_max[i % 2][:].rearrange("p (h k) -> p h k", h=2),
                                AX_X, ALU.max).then_inc(s["max_done"], 1)

            def split_max(name, b, mx, mneg, n):
                st = Steps(dve, name, 2 * b)
                st.then(v.tensor_scalar(mneg[:, :, 0:n], mx[:], -1.0, None, ALU.mult))
                st.inc(v.scalar_tensor_tensor(mneg[:, :, n:2 * n], mx[:], -1.0, mneg[:, :, 0:n],
                                              ALU.mult, ALU.subtract))

            def normalise(st, rsum, att, d, w):
                pv = ps_post[:].rearrange("p (n w) -> p n w", w=w)
                n = rsum.shape[1]
                st.then(v.reciprocal(rsum[:], pv[:, :, d]))
                st.then(v.tensor_tensor(att[:], pv[:, :, 0:d], rsum[:].unsqueeze(2).to_broadcast([P, n, d]), ALU.mult))

            def xmax_tile(b, i):
                dve.wait_ge(s["xmax_ready"], 4 * b + i + 1)
                qt, hh = divmod(i, 2)
                v.tensor_reduce(mx2[:, qt, 8 * hh:8 * hh + 8],
                                ps_max[(i + 1) % 2][:].rearrange("p (h k) -> p h k", h=8),
                                AX_X, ALU.max).then_inc(s["xmax_done"], 1)

            def statistics(st, y, stt, mv):
                for qt in range(QT):
                    st.inc(v.bn_stats(stt[:, qt, :], y[:, qt, :]))
                st.wait()
                for qt in range(QT):
                    st.inc(v.bn_aggr(mv[:, qt, :], stt[:, qt, :]))

            def apply_norm(st, x, b, y, mv, rs):
                for qt in range(QT):
                    st.inc(v.tensor_scalar(x[:, qt, :], y[:, qt, :], mv[:, qt, 0:1], rs[:, qt:qt + 1],
                                           ALU.subtract, ALU.mult))

            def step(b):
                b0, b1, b2, b3, b4 = b
                if on(b1):
                    for i in range(4):
                        max_tile(b1, i)
                if on(b2):
                    ln1 = Steps(dve, "ln1", LN_STEPS * b2)
                    dve.wait_ge(s["o1T_ready"], b2 + 1)
                    normalise(ln1, rsum1, att1, DH1, 32)
                if on(b1):
                    for i in range(4, 8):
                        max_tile(b1, i)
                    dve.wait_ge(s["max_done"], H1 * (b1 + 1))
                    split_max("m_split", b1, mx1, mneg1, H1)
                    dve.wait_ge(s["v_ready"], b1 + 1)
                    if on(b2):
                        dve.wait_ge(s["pv1_done"], 2 * (b2 + 1))
                    v.tensor_copy(vaug[:, :, :, 0:DH1].rearrange("p q h d -> p (q h) d"),
                                  ps_in[:, 0:S].rearrange("p (n d) -> p n d", d=DH1)).then_inc(s["v_kept"], 1)
                if on(b4):
                    ln2 = Steps(dve, "ln2", LN_STEPS * b4)
                    dve.wait_ge(s["o2T_ready"], b4 + 1)
                    normalise(ln2, rsum2, att2, DH2, 16)
                if on(b3):
                    xmax_tile(b3, 0)
                if on(b2):
                    if isinstance(b2, int) and b2 == 0:
                        dve.wait_ge(s["res_set"], 1)
                    ln1.then(v.tensor_tensor(y1[:], att1[:].rearrange("p (q h) d -> p q (h d)", q=QT),
                                             tiles_of(xres, b2), ALU.add))
                    statistics(ln1, y1, st1, mv1)
                if on(b3):
                    xmax_tile(b3, 1)
                if on(b4):
                    dve.wait_ge(s["wo_ready"], b4 + 1)
                    dve.wait_ge(s["res1"], b4 + 1)
                    ln2.then(v.tensor_tensor(y2[:], ps_post[:, S:2 * S].rearrange("p (q d) -> p q d", q=QT),
                                             tiles_of(xres, b4), ALU.add))
                if on(b3):
                    xmax_tile(b3, 2)
                if on(b2):
                    dve.wait_ge(s["rstd1"], 2 * (b2 + 1))
                    apply_norm(ln1, x1, b2, y1, mv1, rs1)
                if on(b3):
                    xmax_tile(b3, 3)
                if on(b4):
                    statistics(ln2, y2, st2, mv2)
                if on(b3):
                    dve.wait_ge(s["xmax_done"], 4 * (b3 + 1))
                    split_max("m2_split", b3, mx2, mneg2, H2)
                if on(b4):
                    dve.wait_ge(s["rstd2"], 2 * (b4 + 1))
                    apply_norm(ln2, x2, b4, y2, mv2, rs2)
                if last_step(b4):
                    dve.wait_ge(s["loaded_router"], 48)
                    rank_logits(r, 0, NT - QT)
                if on(b3):
                    if on(b4):
                        dve.wait_ge(s["pv2_done"], 2 * (b4 + 1))
                    else:
                        dve.wait_ge(s["v2_kept"], 4)
                        dve.wait_ge(s["ones_set"], 2)
                    v.tensor_copy(k2cur[:], k2S[:, :, bass.ds(b3 * SK, SK)]).then_inc(s["k2cur_set"], 1)
                    v.tensor_copy(v2cur[:], v2aug[:, b3, :, :]).then_inc(s["v2cur_set"], 1)

            r = Steps(dve, "route")

            def rank_logits(r, n0, n1):
                dve.wait_ge(s["lg_ready"], 3 if n0 == 0 else 4)
                r.then(v.tensor_tensor(logits[:, n0:n1, :], ps_in[:, n0 * E:n1 * E].rearrange("p (n e) -> p n e", e=E),
                                       ebB[:].unsqueeze(1).to_broadcast([P, n1 - n0, E]), ALU.add))
                for n in range(n0, n1):
                    r.inc(v.max(top[:, n, :], logits[:, n, :]))
                r.wait()
                for n in range(n0, n1):
                    r.inc(v.max_index(topi[:, n, :], top[:, n, :], logits[:, n, :]))

            pipeline(dve, step)

            rank_logits(r, NT - QT, NT)
            r.inc(v.tensor_tensor(gap[:], top[:, :, 1], top[:, :, 0], ALU.subtract))
            r.wait()
            r.inc(v.tensor_copy(topf[:], topi[:, :, 0:2]))
            dve.wait_ge(s["gap_exp"], 1)
            r.then(v.tensor_scalar(den[:], rw[:, :, 1], 1.0, None, ALU.add))
            r.then(v.reciprocal(rw[:, :, 0], den[:]))
            r.then(v.tensor_tensor(rw[:, :, 1], rw[:, :, 1], rw[:, :, 0], ALU.mult))
            for k, dst in ((0, cw[:, :, 0:E]), (1, pick[:])):
                r.then(v.tensor_tensor(dst, iotaE[:].unsqueeze(1).to_broadcast([P, NT, E]),
                                       topf[:, :, k:k + 1].to_broadcast([P, NT, E]), ALU.is_equal))
                r.then(v.tensor_tensor(dst, dst, rw[:, :, k:k + 1].to_broadcast([P, NT, E]), ALU.mult))
            r.then(v.tensor_tensor(cw[:, :, 0:E], cw[:, :, 0:E], pick[:], ALU.add))

            lins = [ps_exp[1], ps_pv]
            down = [ps_max[0], ps_max[1]]

            def accumulate(g, e):
                dve.wait_ge(s["down_ready"], g * NE + e + 1)
                if not (isinstance(g, int) and e == 0):
                    dve.wait_ge(s["acc_done"], g * NE + e)
                for q in range(GT // P):
                    n = g * (GT // P) + q
                    m = v.scalar_tensor_tensor(acc[:, n, :], down[e % 2][:, q * P:(q + 1) * P], cw[:, n, e:e + 1],
                                               acc[:, n, :], ALU.mult, ALU.add)
                m.then_inc(s["acc_done"], 1)

            def last_norm(g):
                ln3 = Steps(dve, "ln3", LN3_STEPS * g)
                wait_alone(dve, s["acc_done"], NE * (g + 1), s["carrier"])
                for q in range(GQ):
                    ln3.inc(v.bn_stats(st3[:, q, :], acc[:, g * GQ + q, :]))
                ln3.wait()
                for q in range(GQ):
                    ln3.inc(v.bn_aggr(mv3[:, q, :], st3[:, q, :]))
                wait_alone(dve, s["rstd3"], 2 * (g + 1), s["carrier"])
                for q in range(GQ):
                    ln3.inc(v.tensor_scalar(yout[:, g * GQ + q, :], acc[:, g * GQ + q, :], mv3[:, q, 0:1],
                                            rs3[:, q:q + 1], ALU.subtract, ALU.mult))

            def products(g):
                for e in range(NE):
                    if not (isinstance(g, int) and e < 2):
                        dve.wait_ge(s["down_ready"], g * NE + e - 1)
                    for c in range(CH):
                        dve.wait_ge(s["silu_done"], (g * NE + e) * CH + c + 1)
                        v.tensor_tensor(hid[:, (e % 2) * CH + c, :], silu[:, c, :], lins[c][:], ALU.mult)\
                            .then_inc(s["hid_done"], 1)
                    if e >= 1:
                        accumulate(g, e - 1)
                    if e == 2 and not isinstance(g, int):
                        last_norm(g - 1)
                accumulate(g, NE - 1)

            dve.wait_ge(s["acc_set"], B)
            products(0)
            with dve.Fori(1, NG) as g:
                products(g)
            last_norm(NG - 1)


def kernel(**inputs):
    import numpy as np
    import concourse.bacc as bacc
    from concourse.bass_utils import run_bass_kernel_spmd

    i = {k: np.asarray(v) for k, v in inputs.items()}
    c = np.ascontiguousarray
    f = np.float32

    def rows(w):
        return w.reshape(2, P, DH1).transpose(1, 0, 2)

    a = {}
    x = i["x"].reshape(B * S, D)
    a["x"] = c(x)
    a["xT"] = c(x.T)
    a["lowV"] = c(np.stack([rows(i["L0_attn_V" + n]) for n in "qkv"], axis=1))
    a["lowU"] = c(np.stack([rows(i["L0_attn_U" + n].transpose(0, 2, 1)) for n in "qkv"], axis=1))
    a["bqk"] = c(np.stack([i["L0_attn_bq"].T.reshape(D), i["L0_attn_bk"].T.reshape(D)], axis=1))
    a["bv1"] = c(i["L0_attn_bv"].reshape(D))
    dh = np.arange(D).reshape(H2, DH2).T.reshape(D)
    a["wx"] = c(np.stack([i["L0_xattn_W" + n][:, dh if n in "qk" else slice(None)] for n in "qkvo"], axis=1))
    a["bx"] = c(np.stack([i["L0_xattn_b" + n][dh if n in "qk" else slice(None)] for n in "qkv"], axis=1))
    a["bo"] = c(i["L0_xattn_bo"])
    a["ctxT"] = c(i["ctx_1024"].reshape(B * SK, D).T)
    a["maskT"] = c(i["mask_SxS2_bk0"].T)
    a["rwT"] = c(i["L0_ffn_router_w"].T)
    a["ebias"] = c(i["L0_ffn_experts_bias"])
    for n in ("", "s"):
        a[n + "w13"] = c(np.stack([i["L0_ffn_" + n + w].transpose(1, 0, 2) for w in ("w1", "w3")], axis=2))
    for n in ("w2", "sw2"):
        w = i["L0_ffn_" + n]
        a[n] = c(w.reshape(w.shape[0], CH, P, D).transpose(2, 0, 1, 3))
    a["ident"] = np.eye(P, dtype=f)
    hm = np.zeros((P, 2, H1), f)
    for p in range(P):
        for ch in range(2):
            hm[p, ch, (ch * P + p) // R1] = 1
    a["headmask"] = hm
    a["onesrow"] = np.full((2, H2 * B * SK // 2), 0x3F803F80, np.uint32).view(f)
    a["iotaE"] = np.tile(np.arange(E, dtype=f), (P, 1))

    nc = bacc.Bacc("TRN2", target_bir_lowering=False, num_devices=1)
    t = {n: nc.dram_tensor("in_" + n, v.shape, mybir.dt.from_np(v.dtype), kind="ExternalInput").ap()
         for n, v in a.items()}
    t["out"] = nc.dram_tensor("out", [B * S, D], F32, kind="ExternalOutput").ap()
    decoder_kernel(nc, t)
    r = run_bass_kernel_spmd(nc, [{"in_" + n: v for n, v in a.items()}], core_ids=[0])
    return r.results[0]["out"].reshape(B, S, D)
```

```python
from contextlib import ExitStack

import concourse.bass as bass
from concourse import mybir
from concourse.alu_op_type import AluOpType as ALU

F32 = mybir.dt.float32
F32R = mybir.dt.float32r
BF16 = mybir.dt.bfloat16
U32 = mybir.dt.uint32
U8 = mybir.dt.uint8
ACT = mybir.ActivationFunctionType
AX_X = mybir.AxisListType.X

P = 128
B, S, D = 8, 256, 128
QT = S // P
NT = B * QT
H1, DH1, R1 = 8, 16, 32
H2, DH2, SK = 16, 8, 64
PAIRS = H2 // 2
E, HF = 8, 256
CH = HF // P
GT = 512
NG = B * S // GT
GQ = GT // P
NE = E + 1
EPS = 1e-5
SCALE1 = 1.0 / DH1 ** 0.5
SCALE2 = 1.0 / DH2 ** 0.5
MASKED = -(2.0 ** 100)

TERMS = [3, 2, 1]
NTERM = sum(TERMS)
K1 = NTERM * DH1
M1 = K1
K1M = K1 + 2
C2 = SK
K2 = SK + NTERM * DH2
K2M = K2 + 2

ROUTED = [(0, NT - QT), (NT - QT, NT)]
SPLIT_STEPS = 3
LN_STEPS = 9
LN_STATS = 7
LN3_STEPS = 3 * GQ
STAGES = 5
FIRST_FULL, LAST_FULL = STAGES, B - 1
N_STEPS = B + STAGES - 1


def pipeline(eng, step):
    def at(s):
        return [s - k if 0 <= s - k < B else None for k in range(STAGES)]

    for s in range(FIRST_FULL):
        step(at(s))
    with eng.Fori(FIRST_FULL, LAST_FULL + 1) as s:
        step([s - k for k in range(STAGES)])
    for s in range(LAST_FULL + 1, N_STEPS):
        step(at(s))


def on(b):
    return b is not None


def last_step(b4):
    return isinstance(b4, int) and b4 == B - 1


def wait_alone(eng, sem, value, carrier):
    eng.wait_ge(sem, value)
    if not isinstance(value, int):
        eng.sem_inc(carrier, 1)


def decoder_kernel(nc, t):
    ctx = ExitStack()
    with ctx:
        def sb(name, shape, dt=F32):
            return ctx.enter_context(nc.sbuf_tensor(name, shape, dt))

        def pb(name, shape, dt=F32):
            return ctx.enter_context(nc.psum_tensor(name, shape, dt))

        def sem(name):
            return ctx.enter_context(nc.semaphore(name))

        ident = sb("ident", [P, P])
        identb = sb("identb", [P, P], BF16)
        headmask = sb("headmask", [P, 2, H1])
        lowV = sb("lowV", [P, 3, 2, DH1])
        lowU = sb("lowU", [P, 3, 2, DH1])
        wqkv = sb("wqkv", [P, 3, P])
        bqk = sb("bqk", [P, 2])
        bvB = sb("bvB", [P, P])
        boB = sb("boB", [P, P])
        wx = sb("wx", [P, 4, P])
        bx = sb("bx", [P, 3])
        ctxT = sb("ctxT", [P, B * SK])
        maskT = sb("maskT", [SK, S], U8)
        maskneg = sb("maskneg", [SK, S], BF16)
        neghalf = sb("neghalf", [P, QT])
        xTv = sb("xTv", [P, S])
        xT = sb("xT", [P, S])
        xres = sb("xres", [P, NT, P])
        x1 = sb("x1", [P, QT, P])
        x2 = sb("x2", [P, QT, P])
        x2T = sb("x2T", [P, B * S])
        x2Th = sb("x2Th", [P, B * S], F32R)
        x2Tl = sb("x2Tl", [P, B * S], F32R)
        qk32 = sb("qk32", [P, 2 * S])
        qkparts = sb("qkparts", [P, 2, 3, S], BF16)
        qkrest = sb("qkrest", [P, 2 * S])
        q2_32 = sb("q2_32", [P, S])
        q2parts = sb("q2parts", [P, 3, S], BF16)
        q2rest = sb("q2rest", [P, S])
        qS = sb("qS", [K1M, 2, H1, S], BF16)
        kS = sb("kS", [K1M, 2, H1, S], BF16)
        q2S = sb("q2S", [K2M, H2, S], BF16)
        k2S = sb("k2S", [K2M, H2, B * SK], BF16)
        k2cur = sb("k2cur", [K2M, H2, SK], BF16)
        vaug = sb("vaug", [P, QT, H1, 32])
        v2aug = sb("v2aug", [P, B, PAIRS, 32])
        v2cur = sb("v2cur", [P, PAIRS, 32])
        probs1 = sb("probs1", [P, H1, 2 * S])
        probs2 = sb("probs2", [P, 4, 2 * S])
        k2_32 = sb("k2_32", [P, B * SK])
        k2rest = sb("k2rest", [P, B * SK])
        k2parts = sb("k2parts", [P, 3, B * SK], BF16)
        bdV, bdU = (probs2[:].rearrange("p a q -> p (a q)")[:, i * 6 * P:(i + 1) * 6 * P]
                    .rearrange("p (i c d) -> p i c d", i=3, c=2) for i in range(2))
        mx1 = sb("mx1", [P, QT, H1])
        mx2 = sb("mx2", [P, QT, H2])
        mneg1 = sb("mneg1", [P, QT, 2 * H1], BF16)
        mneg2 = sb("mneg2", [P, QT, 2 * H2], BF16)
        mrow1 = sb("mrow1", [2 * H1, S], BF16)
        mrow2 = sb("mrow2", [2 * H2, S], BF16)
        o1s = sb("o1s", [P, 2, S])
        o2s = sb("o2s", [P, 2, S])
        rsum1 = sb("rsum1", [P, QT * H1])
        rsum2 = sb("rsum2", [P, QT * H2])
        att1 = sb("att1", [P, QT * H1, DH1])
        att2 = sb("att2", [P, QT * H2, DH2])
        att2T = sb("att2T", [P, S])
        y1 = sb("y1", [P, QT, P])
        y2 = sb("y2", [P, QT, P])
        st1 = sb("st1", [P, QT, 6])
        st2 = sb("st2", [P, QT, 6])
        mv1 = sb("mv1", [P, QT, 2])
        mv2 = sb("mv2", [P, QT, 2])
        ve1 = sb("ve1", [P, QT])
        ve2 = sb("ve2", [P, QT])
        rs1 = sb("rs1", [P, QT])
        rs2 = sb("rs2", [P, QT])
        x1Ts = sb("x1Ts", [P, S])
        w13 = sb("w13", [P, 3, 2, HF])
        w13h = sb("w13h", [P, NE, 2, HF], F32R)
        w13l = sb("w13l", [P, NE, 2, HF], F32R)
        w2 = sb("w2", [P, NE, CH, P])
        rwT = sb("rwT", [P, E])
        ebB = sb("ebB", [P, E])
        iotaE = sb("iotaE", [P, E])
        logits = sb("logits", [P, NT, E])
        top = sb("top", [P, NT, 8])
        topi = sb("topi", [P, NT, 8], U32)
        topf = sb("topf", [P, NT, 2])
        gap = sb("gap", [P, NT])
        rw = sb("rw", [P, NT, 2])
        den = sb("den", [P, NT])
        pick = sb("pick", [P, NT, E])
        cw = sb("cw", [P, NT, NE])
        hid, silu = probs1[:, 0:2 * CH, :], probs1[:, 2 * CH:2 * CH + 2, :]
        acc = xres
        yout = probs2[:].rearrange("p a (m d) -> p (a m) d", d=P)
        st3 = sb("st3", [P, GQ, 6])
        mv3 = sb("mv3", [P, GQ, 2])
        ve3 = sb("ve3", [P, GQ])
        rs3 = sb("rs3", [P, GQ])
        nh3 = sb("nh3", [P, GQ])

        ps_max = [pb(f"ps_max{i}", [P, 512]) for i in range(2)]
        ps_exp = [pb(f"ps_exp{i}", [P, 512]) for i in range(3)]
        ps_pv = pb("ps_pv", [P, 512])
        ps_in = pb("ps_in", [P, 512])
        ps_post = pb("ps_post", [P, 512])

        dram_qk = nc.dram_tensor("qk_parts", [B, 2, 3, P, S], BF16).ap()
        dram_q2 = nc.dram_tensor("q2_parts", [B, 3, P, S], BF16).ap()
        dram_k2 = nc.dram_tensor("k2_parts", [3, P, B * SK], BF16).ap()

        names = """loaded_low loaded_bqk loaded_ident w_split x2T_split loaded_wx loaded_x loaded_xv loaded_res loaded_ffn loaded_shared loaded_router w_high
            consts_set ones_set bd_built w_ready w_kept k2_ready k2_kept k2_split k2_out k2_stacked v2_ready v2_kept
            mask_set rows_set rows_loaded res_set
            qk_ready qk_kept qk_split qk_out qk_stacked v_ready v_kept
            max_ready max_done m_split mT_ready mT_kept m_stacked
            sc_ready exp_done pv1_done o1_kept o1T_ready ln1 rstd1 res1 k2cur_set v2cur_set acc_set x1T_ready x1T_kept
            q2_ready q2_kept q2_split q2_out q2_stacked
            xmax_ready xmax_done m2_split m2T_ready m2T_kept m2_stacked
            xsc_ready xexp_done pv2_done o2_kept o2T_ready ln2 att2T_ready att2T_kept wo_ready rstd2
            x2T_ready x2T_kept
            lg_ready route gap_exp route_last up_ready silu_done hid_done down_ready acc_done ln3 rstd3 stored carrier""".split()
        s = {n: sem(n) for n in names}

        block = ctx.enter_context(nc.Block())

        class Steps:
            def __init__(self, eng, name, base=0):
                self.eng, self.sem, self.base, self.k = eng, s[name], base, 0

            def inc(self, ins):
                ins.then_inc(self.sem, 1)
                self.k += 1

            def wait(self):
                wait_alone(self.eng, self.sem, self.base + self.k, s["carrier"])

            def then(self, ins):
                self.inc(ins)
                self.wait()

        def tiles_of(buf, b):
            return buf[:, bass.ds(b * QT, QT), :]

        def tokens_of(buf, b, n=S):
            return buf[:, bass.ds(b * n, n)]

        @block.sync
        def _(sp):
            def load(dst, src, name):
                sp.dma_start(dst, src).then_inc(s[name], 16)

            load(lowV[:], t["lowV"], "loaded_low")
            load(lowU[:], t["lowU"], "loaded_low")
            load(headmask[:], t["headmask"], "loaded_low")
            load(bqk[:], t["bqk"], "loaded_bqk")
            load(xT[:], t["xT"][:, 0:S], "loaded_x")
            load(ident[:], t["ident"], "loaded_ident")
            load(maskT[:], t["maskT"], "loaded_ident")
            load(wx[:], t["wx"], "loaded_wx")
            load(bx[:], t["bx"], "loaded_wx")
            load(ctxT[:], t["ctxT"], "loaded_wx")
            load(xres[:], t["x"].rearrange("(n p) d -> p n d", p=P), "loaded_res")
            load(bvB[:], t["bv1"].partition_broadcast(P), "loaded_res")
            load(boB[:], t["bo"].partition_broadcast(P), "loaded_res")

            load(kS[M1:K1M, :, :, :].rearrange("p a h t -> p (a h t)").bitcast(F32), t["onesrow"][:, 0:H1 * S],
                 "rows_loaded")
            load(k2S[K2:K2M, :, :].rearrange("p h t -> p (h t)").bitcast(F32), t["onesrow"], "rows_loaded")

            def stack_q(rows, parts, dh, name):
                at = 0
                for a, n in enumerate(TERMS):
                    src = parts[a].rearrange("(d h) t -> d (h t)", d=dh)
                    load(rows(at * dh, n * dh), src.unsqueeze(0).to_broadcast([n, dh, src.shape[1]]), name)
                    at += n

            def stack_k(rows, parts, dh, name):
                at = 0
                for n in TERMS:
                    load(rows(at * dh, n * dh), parts[0:n].rearrange("a (d h) t -> (a d) (h t)", d=dh), name)
                    at += n

            def rows_of(buf, first=0):
                return lambda at, n: buf[first + at:first + at + n].rearrange("p h t -> p (h t)")

            def step(b):
                b0, b1, b2, b3, b4 = b
                if on(b3):
                    wait_alone(sp, s["q2_out"], 16 * (b3 + 1), s["carrier"])
                    if on(b4):
                        wait_alone(sp, s["xsc_ready"], 4 * (b4 + 1), s["carrier"])
                    stack_q(rows_of(q2S, C2), dram_q2[b3], DH2, "q2_stacked")
                if on(b0):
                    wait_alone(sp, s["qk_ready"], b0 + 1, s["carrier"])
                    load(xT[:], t["xT"][:, bass.ds((b0 + 1) % B * S, S)], "loaded_x")
                if on(b0):
                    wait_alone(sp, s["qk_split"], SPLIT_STEPS * (b0 + 1), s["carrier"])
                    load(dram_qk[b0].rearrange("j a p t -> p (j a) t"),
                         qkparts[:].rearrange("p j a t -> p (j a) t"), "qk_out")
                if on(b1):
                    wait_alone(sp, s["mT_kept"], b1 + 1, s["carrier"])
                    load(qS[M1:M1 + 2, b1 % 2, :, :].rearrange("p h t -> p (h t)"), mrow1[:], "m_stacked")
                if on(b0):
                    wait_alone(sp, s["qk_out"], 16 * (b0 + 1), s["carrier"])
                    if not isinstance(b0, int) or b0 >= 2:
                        wait_alone(sp, s["sc_ready"], H1 * (b0 - 1), s["carrier"])
                    stack_q(rows_of(qS[:, b0 % 2]), dram_qk[b0, 0], DH1, "qk_stacked")
                    stack_k(rows_of(kS[:, b0 % 2]), dram_qk[b0, 1], DH1, "qk_stacked")
                if on(b0):
                    if on(b1):
                        wait_alone(sp, s["v_ready"], b1 + 1, s["carrier"])
                    load(xTv[:], t["xT"][:, bass.ds(b0 * S, S)], "loaded_xv")
                if on(b3):
                    wait_alone(sp, s["m2T_kept"], b3 + 1, s["carrier"])
                    load(q2S[K2:K2 + 2, :, :].rearrange("p h t -> p (h t)"), mrow2[:], "m2_stacked")
                if on(b2):
                    wait_alone(sp, s["q2_split"], SPLIT_STEPS * (b2 + 1), s["carrier"])
                    load(dram_q2[b2].rearrange("a p t -> p a t"), q2parts[:], "q2_out")
                if isinstance(b0, int) and b0 == 1:
                    sp.wait_ge(s["k2_split"], SPLIT_STEPS)
                    load(dram_k2.rearrange("a p t -> p a t"), k2parts[:], "k2_out")
                    sp.wait_ge(s["k2_out"], 16)
                    stack_k(rows_of(k2S, C2), dram_k2, DH2, "k2_stacked")

            pipeline(sp, step)
            outv = t["out"].rearrange("(n p) d -> p n d", p=P)
            with sp.Fori(0, NG) as g:
                wait_alone(sp, s["ln3"], LN3_STEPS * (g + 1), s["carrier"])
                load(outv[:, bass.ds(g * GQ, GQ), :], yout[:, bass.ds(g * GQ, GQ), :], "stored")
            sp.wait_ge(s["stored"], 16 * NG)

        @block.gpsimd
        def _(pool):
            g = nc.gpsimd
            g.memset(vaug[:], 0.0).then_inc(s["rows_set"], 1)
            g.memset(v2aug[:], 0.0).then_inc(s["rows_set"], 1)
            pool.wait_ge(s["rows_set"], 2)
            g.memset(vaug[:, :, :, DH1:DH1 + 1], 1.0).then_inc(s["rows_set"], 1)
            g.memset(neghalf[:], -0.5).then_inc(s["rows_set"], 1)
            g.memset(nh3[:], -0.5).then_inc(s["rows_set"], 1)
            g.memset(cw[:, :, E:NE], 1.0).then_inc(s["rows_set"], 1)

            def load_expert(e, slot, w13_src, w2_src, name):
                pool.dma_start(w13[:, slot], w13_src).then_inc(s[name], 16)
                pool.dma_start(w2[:, e], w2_src).then_inc(s[name], 16)

            def split_expert(e, slot, k):
                wait_alone(pool, s["w_high"], k + 1, s["carrier"])
                g.tensor_tensor(w13l[:, e], w13[:, slot], w13h[:, e], ALU.subtract).then_inc(s["w_split"], 1)

            pool.dma_start(rwT[:], t["rwT"]).then_inc(s["loaded_router"], 16)
            pool.dma_start(ebB[:], t["ebias"].partition_broadcast(P)).then_inc(s["loaded_router"], 16)
            pool.dma_start(iotaE[:], t["iotaE"]).then_inc(s["loaded_router"], 16)

            def split(st, src, hi, mid, lo, rest):
                st.inc(g.tensor_tensor(mid, src, hi, ALU.subtract))
                st.then(g.tensor_tensor(rest, src, hi, ALU.subtract))
                st.then(g.tensor_tensor(lo, rest, mid, ALU.subtract))

            def split_k2():
                pool.wait_ge(s["k2_kept"], 2)
                split(Steps(pool, "k2_split"), k2_32[:], *(k2parts[:, a, :] for a in range(3)), k2rest[:])

            def add_value_bias():
                pool.wait_ge(s["loaded_res"], 48)
                g.tensor_tensor(xres[:], xres[:], bvB[:].unsqueeze(1).to_broadcast([P, NT, P]),
                                ALU.add).then_inc(s["res_set"], 1)

            def rstd(ln, name, b, mv, ve, rs):
                wait_alone(pool, s[ln], LN_STEPS * b + LN_STATS, s["carrier"])
                st = Steps(pool, name, 2 * b)
                st.then(g.tensor_scalar(ve[:], mv[:, :, 1], EPS, None, ALU.add))
                st.inc(g.tensor_tensor(rs[:], ve[:], neghalf[:], ALU.pow))

            def step(b):
                b0, b1, b2, b3, b4 = b
                if on(b0):
                    wait_alone(pool, s["qk_kept"], b0 + 1, s["carrier"])
                    wait_alone(pool, s["qk_out"], 16 * b0, s["carrier"])
                    split(Steps(pool, "qk_split", SPLIT_STEPS * b0), qk32[:].rearrange("p (j t) -> p j t", j=2),
                          *(qkparts[:, :, a, :] for a in range(3)), qkrest[:].rearrange("p (j t) -> p j t", j=2))
                    if isinstance(b0, int) and b0 == 0:
                        split_k2()
                if on(b1):
                    split_expert(b1, b1 % 2, b1)
                elif isinstance(b2, int) and b2 == B - 1:
                    split_expert(E, 2, E)
                if on(b2):
                    rstd("ln1", "rstd1", b2, mv1, ve1, rs1)
                if on(b0):
                    if isinstance(b0, int) and b0 == 1:
                        add_value_bias()
                        load_expert(E, 2, t["sw13"][:, 0], t["sw2"][:, 0], "loaded_shared")
                    if not isinstance(b0, int) or b0 >= 1:
                        wait_alone(pool, s["loaded_ffn"], 32 * b0, s["carrier"])
                    load_expert(b0, b0 % 2, t["w13"][:, b0], t["w2"][:, b0], "loaded_ffn")
                if on(b4):
                    rstd("ln2", "rstd2", b4, mv2, ve2, rs2)
                if on(b2):
                    wait_alone(pool, s["ln1"], LN_STEPS * (b2 + 1), s["carrier"])
                    g.tensor_tensor(tiles_of(xres, b2), x1[:],
                                    boB[:].unsqueeze(1).to_broadcast([P, QT, P]), ALU.add).then_inc(s["res1"], 1)
                    wait_alone(pool, s["q2_kept"], 2 * (b2 + 1), s["carrier"])
                    wait_alone(pool, s["q2_out"], 16 * b2, s["carrier"])
                    split(Steps(pool, "q2_split", SPLIT_STEPS * b2), q2_32[:], *(q2parts[:, a, :] for a in range(3)),
                          q2rest[:])
                if on(b4):
                    wait_alone(pool, s["ln2"], LN_STEPS * (b4 + 1), s["carrier"])
                    g.tensor_copy(tiles_of(acc, b4), x2[:]).then_inc(s["acc_set"], 1)
                if on(b4):
                    wait_alone(pool, s["x2T_kept"], 2 * (b4 + 1), s["carrier"])
                    g.tensor_tensor(tokens_of(x2Tl, b4), tokens_of(x2T, b4), tokens_of(x2Th, b4),
                                    ALU.subtract).then_inc(s["x2T_split"], 1)

            pipeline(pool, step)
            with pool.Fori(0, NG) as i:
                wait_alone(pool, s["ln3"], LN3_STEPS * i + 2 * GQ, s["carrier"])
                st = Steps(pool, "rstd3", 2 * i)
                st.then(g.tensor_scalar(ve3[:], mv3[:, :, 1], EPS, None, ALU.add))
                st.inc(g.tensor_tensor(rs3[:], ve3[:], nh3[:], ALU.pow))

        @block.tensor
        def _(pe):
            mm = nc.tensor.matmul
            tr = nc.tensor.transpose
            pe.wait_ge(s["bd_built"], 12)
            for i in range(3):
                for c in range(2):
                    m = mm(ps_in[:, i * P:(i + 1) * P], bdV[:, i, c, :], bdU[:, i, c, :], start=c == 0, stop=c == 1)
            m.then_inc(s["w_ready"], 1)
            pe.wait_ge(s["w_kept"], 1)

            def context():
                pe.wait_ge(s["loaded_wx"], 48)
                mm(ps_post[:], wx[:, 1, :], ctxT[:], start=True, stop=True).then_inc(s["k2_ready"], 1)
                for b in range(B):
                    for a in range(2):
                        m = mm(ps_exp[b // 4][64 * a:64 * a + 64, (b % 4) * P:(b % 4 + 1) * P],
                               ctxT[:, b * SK:(b + 1) * SK], wx[:, 2, :], start=True, stop=True,
                               tile_position=(0, 64 * a))
                m.then_inc(s["v2_ready"], 1)

            def max_tile(b, i):
                if i >= 2:
                    pe.wait_ge(s["max_done"], H1 * b + i - 1)
                qt, hp = divmod(i, H1 // 2)
                for j in range(2):
                    h = 2 * hp + j
                    m = mm(ps_max[i % 2][:, j * S:(j + 1) * S], qS[0:K1, b % 2, h, qt * P:(qt + 1) * P],
                           kS[0:K1, b % 2, h, :], start=True, stop=True)
                m.then_inc(s["max_ready"], 1)

            def score_tile(b, h):
                if h >= 3:
                    pe.wait_ge(s["exp_done"], H1 * b + h - 2)
                for kt in range(QT):
                    m = mm(ps_exp[(4 + h) % 3][:, kt * S:(kt + 1) * S], kS[:, b % 2, h, kt * P:(kt + 1) * P],
                           qS[:, b % 2, h, :], start=True, stop=True)
                m.then_inc(s["sc_ready"], 1)

            def pv_group(b, g):
                pe.wait_ge(s["exp_done"], H1 * b + 4 * g + 4)
                for kt in range(QT):
                    for j in range(4):
                        h = 4 * g + j
                        m = mm(ps_pv[32 * j:32 * j + 32, g * S:(g + 1) * S], vaug[:, kt, h, :],
                               probs1[:, h, kt * S:(kt + 1) * S], start=kt == 0, stop=kt == QT - 1,
                               tile_position=(0, 32 * j))
                m.then_inc(s["pv1_done"], 1)

            def xscore_tile(b, i):
                if i == 0:
                    pe.wait_ge(s["k2cur_set"], b + 1)
                if i == 3:
                    pe.wait_ge(s["xexp_done"], 4 * b + 1)
                for pr in range(2):
                    for a in range(2):
                        h = 4 * i + 2 * pr + a
                        m = mm(ps_exp[i % 3][64 * a:64 * a + 64, pr * S:(pr + 1) * S],
                               k2cur[:, h, :], q2S[:, h, :], start=True, stop=True,
                               tile_position=(0, 64 * a))
                m.then_inc(s["xsc_ready"], 1)

            def xpv_group(b, g):
                pe.wait_ge(s["v2cur_set"], b + 1)
                pe.wait_ge(s["xexp_done"], 4 * b + 2 * g + 2)
                for j in range(4):
                    pr = 4 * g + j
                    m = mm(ps_pv[32 * j:32 * j + 32, g * S:(g + 1) * S], v2cur[:, pr, :],
                           probs2[:, pr // 2, (pr % 2) * S:(pr % 2 + 1) * S], start=True, stop=True,
                           tile_position=(0, 32 * j))
                m.then_inc(s["pv2_done"], 1)

            def xmax_tile(b, i):
                if i >= 2:
                    pe.wait_ge(s["xmax_done"], 4 * b + i - 1)
                qt, hh = divmod(i, 2)
                for j in range(8):
                    h = 8 * hh + j
                    m = mm(ps_max[(i + 1) % 2][:, j * SK:(j + 1) * SK], q2S[0:K2, h, qt * P:(qt + 1) * P],
                           k2S[0:K2, h, bass.ds(b * SK, SK)], start=True, stop=True)
                m.then_inc(s["xmax_ready"], 1)

            def transpose_heads(b, src, name):
                for qt in range(QT):
                    for g in range(2):
                        c = (qt * 2 + g) * P
                        m = tr(ps_post[:, c:c + P], src[:, g, qt * P:(qt + 1) * P], ident[:])
                m.then_inc(s[name], 1)

            def router(n0, n1):
                for n in range(n0, n1):
                    m = mm(ps_in[:, n * E:(n + 1) * E], x2T[:, n * P:(n + 1) * P], rwT[:], start=True, stop=True)
                m.then_inc(s["lg_ready"], 1)

            def transpose_tiles(src, name):
                for qt in range(QT):
                    m = tr(ps_post[:, qt * P:(qt + 1) * P], src(qt), ident[:])
                m.then_inc(s[name], 1)

            def keep_busy(n, bank):
                for _ in range(n):
                    mm(bank[:, 0:P], ident[:], ident[:], start=True, stop=True)

            def make_o2T(b2, b4):
                pe.wait_ge(s["o2_kept"], b4 + 1)
                if on(b2):
                    pe.wait_ge(s["ln1"], LN_STEPS * b2 + 2)
                else:
                    pe.wait_ge(s["x2T_kept"], 2 * b4)
                transpose_heads(b4, o2s, "o2T_ready")

            def make_att2T(b4):
                pe.wait_ge(s["ln2"], LN_STEPS * b4 + 2)
                transpose_tiles(lambda qt: att2[:, qt * H2:(qt + 1) * H2, :].rearrange("p h d -> p (h d)"),
                                "att2T_ready")

            def project_out(b4):
                pe.wait_ge(s["att2T_kept"], b4 + 1)
                for qt in range(QT):
                    m = mm(ps_post[:, S + qt * P:S + (qt + 1) * P], att2T[:, qt * P:(qt + 1) * P], wx[:, 3, :],
                           start=True, stop=True)
                m.then_inc(s["wo_ready"], 1)

            def make_x2T(b2, b4):
                if on(b2):
                    pe.wait_ge(s["q2_kept"], 2 * (b2 + 1))
                pe.wait_ge(s["ln2"], LN_STEPS * (b4 + 1))
                transpose_tiles(lambda qt: x2[:, qt, :], "x2T_ready")

            def transpose_max(mneg, n, name):
                for qt in range(QT):
                    m = tr(ps_max[0].bitcast(BF16)[0:n, qt * P:(qt + 1) * P], mneg[:, qt, :], identb[:])
                m.then_inc(s[name], 1)

            def step(b):
                b0, b1, b2, b3, b4 = b
                if on(b0):
                    if on(b1) and (not isinstance(b1, int) or b1 >= 1):
                        pe.wait_ge(s["v_kept"], b1)
                    elif on(b1):
                        pe.wait_ge(s["qk_kept"], 1)
                    pe.wait_ge(s["loaded_x"], 16 * (b0 + 1))
                    for i in range(2):
                        m = mm(ps_in[:, i * S:(i + 1) * S], wqkv[:, i, :], xT[:], start=True, stop=True)
                    m.then_inc(s["qk_ready"], 1)
                    if isinstance(b0, int) and b0 == 0:
                        context()
                if on(b1):
                    pe.wait_ge(s["qk_stacked"], 16 * 6 * (b1 + 1))
                    if on(b3) and (not isinstance(b3, int) or b3 >= 1):
                        pe.wait_ge(s["m2T_kept"], b3)
                    max_tile(b1, 0)
                    max_tile(b1, 1)
                if on(b2):
                    pv_group(b2, 1)
                if last_step(b4):
                    keep_busy(4, ps_exp[0])
                    pe.wait_ge(s["x2T_kept"], 2 * b4)
                    router(NT - 2 * QT, NT - QT)
                    keep_busy(3, ps_exp[0])
                if on(b4) and not on(b1) and not last_step(b4):
                    keep_busy(5, ps_exp[0])
                if on(b4):
                    pe.wait_ge(s["m2_stacked"], 16 * (b4 + 1))
                for i in range(2):
                    if on(b4):
                        xscore_tile(b4, i)
                    if on(b1):
                        max_tile(b1, i + 2)
                if on(b4):
                    xscore_tile(b4, 2)
                if on(b1):
                    max_tile(b1, 4)
                if on(b2):
                    pe.wait_ge(s["o1_kept"], b2 + 1)
                    if not isinstance(b2, int) or b2 >= 1:
                        pe.wait_ge(s["q2_kept"], 2 * b2)
                    if on(b4):
                        pe.wait_ge(s["x2T_kept"], 2 * b4)
                    transpose_heads(b2, o1s, "o1T_ready")
                if on(b4):
                    xscore_tile(b4, 3)
                if on(b1):
                    max_tile(b1, 5)
                if on(b4):
                    xpv_group(b4, 0)
                if on(b1):
                    max_tile(b1, 6)
                if on(b4):
                    xpv_group(b4, 1)
                if on(b1):
                    max_tile(b1, 7)
                if on(b4) and not last_step(b4):
                    make_o2T(b2, b4)
                if on(b1) and on(b2):
                    keep_busy(1 if on(b4) else 2, ps_exp[1])
                if on(b1):
                    pe.wait_ge(s["m_split"], 2 * (b1 + 1))
                    transpose_max(mneg1, 2 * H1, "mT_ready")
                    if on(b0):
                        pe.wait_ge(s["qk_kept"], b0 + 1)
                    pe.wait_ge(s["loaded_xv"], 16 * (b1 + 1))
                    for qt in range(QT):
                        m = mm(ps_in[:, qt * P:(qt + 1) * P], xTv[:, qt * P:(qt + 1) * P], wqkv[:, 2, :],
                               start=True, stop=True)
                    m.then_inc(s["v_ready"], 1)
                if on(b3):
                    if on(b4) and not on(b1):
                        keep_busy(8, ps_exp[1])
                    pe.wait_ge(s["q2_stacked"], 16 * 3 * (b3 + 1))
                    if isinstance(b3, int) and b3 == 0:
                        pe.wait_ge(s["mask_set"], 2)
                        pe.wait_ge(s["k2_stacked"], 16 * 3)
                        pe.wait_ge(s["rows_loaded"], 32)
                    xmax_tile(b3, 0)
                if on(b4) and not last_step(b4):
                    keep_busy(1 if on(b1) else 4, ps_exp[1])
                    make_att2T(b4)
                if on(b3):
                    if on(b1):
                        pe.wait_ge(s["mT_kept"], b1 + 1)
                    xmax_tile(b3, 1)
                if on(b4) and not last_step(b4):
                    project_out(b4)
                if on(b1) and on(b2):
                    keep_busy(1 if on(b4) else 8, ps_exp[1])
                if on(b1):
                    pe.wait_ge(s["m_stacked"], 16 * (b1 + 1))
                    if isinstance(b1, int) and b1 == 0:
                        pe.wait_ge(s["rows_loaded"], 32)
                        pe.wait_ge(s["v2_kept"], 4)
                    score_tile(b1, 0)
                    score_tile(b1, 1)
                if on(b3):
                    xmax_tile(b3, 2)
                if on(b1):
                    score_tile(b1, 2)
                    score_tile(b1, 3)
                if on(b3):
                    xmax_tile(b3, 3)
                if on(b2):
                    if on(b4):
                        pe.wait_ge(s["ln2"], LN_STEPS * b4 + 3)
                    pe.wait_ge(s["ln1"], LN_STEPS * (b2 + 1))
                    transpose_tiles(lambda qt: x1[:, qt, :], "x1T_ready")
                if on(b1):
                    score_tile(b1, 4)
                    score_tile(b1, 5)
                if on(b3) and on(b1):
                    pe.wait_ge(s["m2_split"], 2 * (b3 + 1))
                    transpose_max(mneg2, 2 * H2, "m2T_ready")
                if on(b2):
                    pe.wait_ge(s["x1T_kept"], b2 + 1)
                    mm(ps_post[:, S:2 * S], wx[:, 0, :], x1Ts[:], start=True, stop=True).then_inc(s["q2_ready"], 1)
                if on(b1):
                    score_tile(b1, 6)
                    pe.wait_ge(s["v_kept"], b1 + 1)
                    if isinstance(b1, int) and b1 == 0:
                        pe.wait_ge(s["rows_set"], 3)
                    if on(b4):
                        pe.wait_ge(s["o2_kept"], b4 + 1)
                    pv_group(b1, 0)
                if isinstance(b4, int) and b4 == B - 2:
                    pe.wait_ge(s["loaded_router"], 48)
                    router(0, 6)
                if on(b3) and on(b4) and not on(b1):
                    keep_busy(3, ps_exp[1])
                if on(b3) and not on(b1):
                    pe.wait_ge(s["m2_split"], 2 * (b3 + 1))
                    transpose_max(mneg2, 2 * H2, "m2T_ready")
                if on(b1):
                    score_tile(b1, 7)
                if on(b4) and not last_step(b4):
                    if isinstance(b4, int) and b4 == B - 2:
                        router(6, NT - 2 * QT)
                    make_x2T(b2, b4)

            pipeline(pe, step)

            up = [(ps_exp[0], ps_exp[1]), (ps_exp[2], ps_pv)]
            down = [ps_max[0], ps_max[1]]

            def up_unit(g, u):
                gate, lin = up[u % 2]
                if not (isinstance(g, int) and u < 2):
                    pe.wait_ge(s["hid_done"], g * NE * CH + u - 1)
                e, c = divmod(u, CH)
                xh, xl = x2Th[:, bass.ds(g * GT, GT)], x2Tl[:, bass.ds(g * GT, GT)]
                for i, out in ((0, gate), (1, lin)):
                    for j, (w, x) in enumerate(((w13l, xh), (w13h, xl), (w13h, xh))):
                        m = mm(out[:], w[:, e, i, c * P:(c + 1) * P], x, start=j == 0, stop=j == 2)
                m.then_inc(s["up_ready"], 1)

            def down_unit(g, e):
                n = g * NE + e
                pe.wait_ge(s["hid_done"], (n + 1) * CH)
                if not (isinstance(g, int) and e < 2):
                    pe.wait_ge(s["acc_done"], n - 1)
                for q in range(GT // P):
                    for c in range(CH):
                        m = mm(down[e % 2][:, q * P:(q + 1) * P], hid[:, (e % 2) * CH + c, q * P:(q + 1) * P],
                               w2[:, e, c, :], start=c == 0, stop=c == CH - 1)
                m.then_inc(s["down_ready"], 1)

            def group(g):
                pe.wait_ge(s["x2T_split"], GT // S * (g + 1))
                for e in range(NE):
                    for c in range(CH):
                        up_unit(g, e * CH + c)
                        if not isinstance(g, int):
                            continue
                        if (e, c) == (0, 0):
                            make_o2T(None, B - 1)
                        if (e, c) == (0, 1):
                            make_att2T(B - 1)
                        if (e, c) == (1, 0):
                            project_out(B - 1)
                        if (e, c) == (2, 0):
                            make_x2T(None, B - 1)
                        if (e, c) == (3, 1):
                            pe.wait_ge(s["x2T_kept"], 2 * B)
                            pe.wait_ge(s["route"], 1)
                            router(NT - QT, NT)
                    if e >= 1:
                        down_unit(g, e - 1)
                down_unit(g, NE - 1)

            pe.wait_ge(s["loaded_ffn"], 32 * E)
            pe.wait_ge(s["loaded_shared"], 32)
            pe.wait_ge(s["w_split"], NE)
            keep_busy(4, ps_exp[0])
            pe.wait_ge(s["o2_kept"], B)
            group(0)
            with pe.Fori(1, NG) as g:
                group(g)

        @block.scalar
        def _(act):
            a = nc.scalar.activation

            def copy(out, in_, name, bias=None):
                if bias is None:
                    a(out, in_, ACT.Copy).then_inc(s[name], 1)
                else:
                    a(out, in_, ACT.Identity, bias=bias).then_inc(s[name], 1)

            act.wait_ge(s["w_ready"], 1)
            copy(wqkv[:].rearrange("p i d -> p (i d)"), ps_in[:, 0:3 * P], "w_kept")

            def high_part(e, slot, k):
                if isinstance(k, int) and k == E:
                    act.wait_ge(s["loaded_shared"], 32)
                else:
                    act.wait_ge(s["loaded_ffn"], 32 * (k + 1))
                copy(w13h[:, e], w13[:, slot], "w_high")

            def keep_att2T(b4):
                act.wait_ge(s["att2T_ready"], b4 + 1)
                copy(att2T[:], ps_post[:, 0:S], "att2T_kept", bx[:, 2:3])

            def keep_x2T(b4):
                act.wait_ge(s["x2T_ready"], b4 + 1)
                copy(tokens_of(x2T, b4), ps_post[:, 0:S], "x2T_kept")
                copy(tokens_of(x2Th, b4), ps_post[:, 0:S], "x2T_kept")

            def exp_gap(k):
                n0, n1 = ROUTED[k]
                name = ("route", "route_last")[k]
                act.wait_ge(s[name], n1 - n0 + 2)
                a(rw[:, n0:n1, 1], gap[:, n0:n1], ACT.Exp).then_inc(s["gap_exp"], 1)

            def exp1(b, h):
                act.wait_ge(s["sc_ready"], H1 * b + h + 1)
                a(probs1[:, h, :], ps_exp[(4 + h) % 3][:], ACT.Exp, scale=SCALE1).then_inc(s["exp_done"], 1)

            def step(b):
                b0, b1, b2, b3, b4 = b
                if on(b0):
                    act.wait_ge(s["qk_ready"], b0 + 1)
                    act.wait_ge(s["qk_split"], SPLIT_STEPS * b0)
                    act.wait_ge(s["qk_out"], 16 * b0)
                    for j in range(2):
                        a(qk32[:, j * S:(j + 1) * S], ps_in[:, j * S:(j + 1) * S], ACT.Identity, bias=bqk[:, j:j + 1])
                        m = a(qkparts[:, j, 0, :], ps_in[:, j * S:(j + 1) * S], ACT.Identity, bias=bqk[:, j:j + 1])
                    m.then_inc(s["qk_kept"], 1)
                    if isinstance(b0, int) and b0 == 0:
                        act.wait_ge(s["k2_ready"], 1)
                        copy(k2_32[:], ps_post[:], "k2_kept", bx[:, 1:2])
                        copy(k2parts[:, 0, :], ps_post[:], "k2_kept", bx[:, 1:2])
                if on(b2):
                    act.wait_ge(s["pv1_done"], 2 * (b2 + 1))
                    copy(o1s[:].rearrange("p g q -> p (g q)"), ps_pv[:], "o1_kept")
                if on(b4):
                    for i in range(4):
                        act.wait_ge(s["xsc_ready"], 4 * b4 + i + 1)
                        a(probs2[:, i, :], ps_exp[i % 3][:], ACT.Exp, scale=SCALE2).then_inc(s["xexp_done"], 1)
                if last_step(b4):
                    exp_gap(0)
                if on(b4):
                    act.wait_ge(s["pv2_done"], 2 * (b4 + 1))
                    copy(o2s[:].rearrange("p g q -> p (g q)"), ps_pv[:], "o2_kept")
                if on(b1):
                    high_part(b1, b1 % 2, b1)
                elif isinstance(b2, int) and b2 == B - 1:
                    high_part(E, 2, E)
                if on(b1):
                    act.wait_ge(s["mT_ready"], b1 + 1)
                    act.wait_ge(s["m_stacked"], 16 * b1)
                    copy(mrow1[:], ps_max[0].bitcast(BF16)[0:2 * H1, 0:S], "mT_kept")
                if on(b4) and not last_step(b4):
                    keep_att2T(b4)
                if on(b1):
                    for h in range(4):
                        exp1(b1, h)
                if on(b2):
                    act.wait_ge(s["x1T_ready"], b2 + 1)
                    copy(x1Ts[:], ps_post[:, 0:S], "x1T_kept")
                if on(b1):
                    exp1(b1, 4)
                    exp1(b1, 5)
                if on(b3) and on(b1):
                    act.wait_ge(s["m2T_ready"], b3 + 1)
                    act.wait_ge(s["m2_stacked"], 16 * b3)
                    copy(mrow2[:], ps_max[0].bitcast(BF16)[0:2 * H2, 0:S], "m2T_kept")
                if on(b2):
                    act.wait_ge(s["q2_ready"], b2 + 1)
                    act.wait_ge(s["q2_split"], SPLIT_STEPS * b2)
                    act.wait_ge(s["q2_out"], 16 * b2)
                    copy(q2_32[:], ps_post[:, S:2 * S], "q2_kept", bx[:, 0:1])
                    copy(q2parts[:, 0, :], ps_post[:, S:2 * S], "q2_kept", bx[:, 0:1])
                if on(b3) and not on(b1):
                    act.wait_ge(s["m2T_ready"], b3 + 1)
                    act.wait_ge(s["m2_stacked"], 16 * b3)
                    copy(mrow2[:], ps_max[0].bitcast(BF16)[0:2 * H2, 0:S], "m2T_kept")
                if on(b1):
                    exp1(b1, 6)
                    exp1(b1, 7)
                if on(b4) and not last_step(b4):
                    keep_x2T(b4)

            pipeline(act, step)
            gates = [ps_exp[0], ps_exp[2]]

            def silus(g):
                for u in range(NE * CH):
                    act.wait_ge(s["up_ready"], g * NE * CH + u + 1)
                    if not (isinstance(g, int) and u < 2):
                        act.wait_ge(s["hid_done"], g * NE * CH + u - 1)
                    a(silu[:, u % 2, :], gates[u % 2][:], ACT.Silu).then_inc(s["silu_done"], 1)
                    if isinstance(g, int) and u == 1:
                        keep_att2T(B - 1)
                    if isinstance(g, int) and u == 4:
                        keep_x2T(B - 1)
                    if isinstance(g, int) and u == 7:
                        exp_gap(1)

            silus(0)
            with act.Fori(1, NG) as g:
                silus(g)

        @block.vector
        def _(dve):
            v = nc.vector
            dve.wait_ge(s["loaded_low"], 48)
            for i in range(3):
                for c in range(2):
                    mask = headmask[:, c, :].unsqueeze(2).to_broadcast([P, H1, DH1])
                    for dst, src in ((bdV, lowV), (bdU, lowU)):
                        order = "p (d h) -> p h d" if dst is bdU and i < 2 else "p (h d) -> p h d"
                        v.tensor_tensor(dst[:, i, c, :].rearrange(order, h=H1),
                                        src[:, i, c, :].unsqueeze(1).to_broadcast([P, H1, DH1]), mask,
                                        ALU.mult).then_inc(s["bd_built"], 1)
            dve.wait_ge(s["loaded_ident"], 32)
            v.tensor_copy(identb[:], ident[:]).then_inc(s["consts_set"], 1)
            v.tensor_scalar(maskneg[:], maskT[:], 0.0, MASKED, ALU.is_equal, ALU.mult).then_inc(s["consts_set"], 1)
            dve.wait_ge(s["consts_set"], 2)
            v.tensor_copy(q2S[0:SK, :, :], maskneg[:].unsqueeze(1).to_broadcast([SK, H2, S]))\
                .then_inc(s["mask_set"], 1)
            v.tensor_copy(k2S[0:SK, :, :].rearrange("p h (b k) -> p (h b) k", b=B),
                          identb[0:SK, 0:SK].unsqueeze(1).to_broadcast([SK, H2 * B, SK])).then_inc(s["mask_set"], 1)
            dve.wait_ge(s["rows_set"], 2)
            v.memset(v2aug[0:64, :, :, DH2:DH2 + 1], 1.0).then_inc(s["ones_set"], 1)
            v.memset(v2aug[64:P, :, :, 16 + DH2:17 + DH2], 1.0).then_inc(s["ones_set"], 1)
            dve.wait_ge(s["v2_ready"], 1)
            for half in range(2):
                for a in range(2):
                    src = ps_exp[half][64 * a:64 * a + 64, :].rearrange("p (n a d) -> p n a d", a=2, d=DH2)
                    dst = v2aug[64 * a:64 * a + 64, 4 * half:4 * half + 4, :, 16 * a:16 * a + DH2]
                    v.tensor_copy(dst.rearrange("p b r d -> p (b r) d"), src[:, :, a, :]).then_inc(s["v2_kept"], 1)

            def max_tile(b, i):
                dve.wait_ge(s["max_ready"], H1 * b + i + 1)
                qt, hp = divmod(i, H1 // 2)
                v.tensor_reduce(mx1[:, qt, 2 * hp:2 * hp + 2], ps_max[i % 2][:].rearrange("p (h k) -> p h k", h=2),
                                AX_X, ALU.max).then_inc(s["max_done"], 1)

            def split_max(name, b, mx, mneg, n):
                st = Steps(dve, name, 2 * b)
                st.then(v.tensor_scalar(mneg[:, :, 0:n], mx[:], -1.0, None, ALU.mult))
                st.inc(v.scalar_tensor_tensor(mneg[:, :, n:2 * n], mx[:], -1.0, mneg[:, :, 0:n],
                                              ALU.mult, ALU.subtract))

            def normalise(st, rsum, att, d, w, between=None):
                pv = ps_post[:].rearrange("p (n w) -> p n w", w=w)
                n = rsum.shape[1]
                st.inc(v.reciprocal(rsum[:], pv[:, :, d]))
                if between:
                    between()
                st.wait()
                st.inc(v.tensor_tensor(att[:], pv[:, :, 0:d], rsum[:].unsqueeze(2).to_broadcast([P, n, d]), ALU.mult))

            def xmax_tile(b, i):
                dve.wait_ge(s["xmax_ready"], 4 * b + i + 1)
                qt, hh = divmod(i, 2)
                v.tensor_reduce(mx2[:, qt, 8 * hh:8 * hh + 8],
                                ps_max[(i + 1) % 2][:].rearrange("p (h k) -> p h k", h=8),
                                AX_X, ALU.max).then_inc(s["xmax_done"], 1)

            def apply_norm(st, x, b, y, mv, rs):
                for qt in range(QT):
                    st.inc(v.tensor_scalar(x[:, qt, :], y[:, qt, :], mv[:, qt, 0:1], rs[:, qt:qt + 1],
                                           ALU.subtract, ALU.mult))

            def route(k):
                n0, n1 = ROUTED[k]
                n = n1 - n0
                r = Steps(dve, ("route", "route_last")[k])
                dve.wait_ge(s["lg_ready"], (3, 4)[k])
                r.then(v.tensor_tensor(logits[:, n0:n1, :], ps_in[:, n0 * E:n1 * E].rearrange("p (n e) -> p n e", e=E),
                                       ebB[:].unsqueeze(1).to_broadcast([P, n, E]), ALU.add))
                for i in range(n0, n1):
                    r.inc(v.max(top[:, i, :], logits[:, i, :]))
                r.wait()
                r.inc(v.tensor_tensor(gap[:, n0:n1], top[:, n0:n1, 1], top[:, n0:n1, 0], ALU.subtract))
                for i in range(n0, n1):
                    r.inc(v.max_index(topi[:, i, :], top[:, i, :], logits[:, i, :]))
                r.wait()
                r.inc(v.tensor_copy(topf[:, n0:n1, :], topi[:, n0:n1, 0:2]))
                dve.wait_ge(s["gap_exp"], k + 1)
                r.then(v.tensor_scalar(den[:, n0:n1], rw[:, n0:n1, 1], 1.0, None, ALU.add))
                r.then(v.reciprocal(rw[:, n0:n1, 0], den[:, n0:n1]))
                r.then(v.tensor_tensor(rw[:, n0:n1, 1], rw[:, n0:n1, 1], rw[:, n0:n1, 0], ALU.mult))
                for j, dst in ((0, cw[:, n0:n1, 0:E]), (1, pick[:, n0:n1, :])):
                    r.then(v.tensor_tensor(dst, iotaE[:].unsqueeze(1).to_broadcast([P, n, E]),
                                           topf[:, n0:n1, j:j + 1].to_broadcast([P, n, E]), ALU.is_equal))
                    r.then(v.tensor_tensor(dst, dst, rw[:, n0:n1, j:j + 1].to_broadcast([P, n, E]), ALU.mult))
                r.then(v.tensor_tensor(cw[:, n0:n1, 0:E], cw[:, n0:n1, 0:E], pick[:, n0:n1, :], ALU.add))

            def norm2_read(b4, between=None):
                ln2 = Steps(dve, "ln2", LN_STEPS * b4)
                dve.wait_ge(s["o2T_ready"], b4 + 1)
                normalise(ln2, rsum2, att2, DH2, 16, between)
                return ln2

            def norm2_add(ln2, b4):
                dve.wait_ge(s["wo_ready"], b4 + 1)
                dve.wait_ge(s["res1"], b4 + 1)
                ln2.inc(v.tensor_tensor(y2[:], ps_post[:, S:2 * S].rearrange("p (q d) -> p q d", q=QT),
                                        tiles_of(xres, b4), ALU.add))

            def stats(st, y, stt):
                st.wait()
                for qt in range(QT):
                    st.inc(v.bn_stats(stt[:, qt, :], y[:, qt, :]))

            def aggregate(st, stt, mv):
                st.wait()
                for qt in range(QT):
                    st.inc(v.bn_aggr(mv[:, qt, :], stt[:, qt, :]))

            def norm2_apply(ln2, b4):
                dve.wait_ge(s["rstd2"], 2 * (b4 + 1))
                apply_norm(ln2, x2, b4, y2, mv2, rs2)

            def keep_v(b1, b2):
                dve.wait_ge(s["v_ready"], b1 + 1)
                if on(b2):
                    dve.wait_ge(s["pv1_done"], 2 * (b2 + 1))
                v.tensor_copy(vaug[:, :, :, 0:DH1].rearrange("p q h d -> p (q h) d"),
                              ps_in[:, 0:S].rearrange("p (n d) -> p n d", d=DH1)).then_inc(s["v_kept"], 1)

            def step(b):
                b0, b1, b2, b3, b4 = b
                if on(b1):
                    for i in range(5):
                        max_tile(b1, i)
                if on(b2):
                    ln1 = Steps(dve, "ln1", LN_STEPS * b2)
                    dve.wait_ge(s["o1T_ready"], b2 + 1)
                    normalise(ln1, rsum1, att1, DH1, 32, (lambda: max_tile(b1, 5)) if on(b1) else None)
                elif on(b1):
                    max_tile(b1, 5)
                if on(b1):
                    max_tile(b1, 6)
                    max_tile(b1, 7)
                    dve.wait_ge(s["max_done"], H1 * (b1 + 1))
                    split_max("m_split", b1, mx1, mneg1, H1)
                if last_step(b4):
                    dve.wait_ge(s["loaded_router"], 48)
                    route(0)
                    return
                if on(b4):
                    ln2 = norm2_read(b4, (lambda: keep_v(b1, b2)) if on(b1) else None)
                elif on(b1):
                    keep_v(b1, b2)
                if on(b3):
                    xmax_tile(b3, 0)
                if on(b2):
                    if isinstance(b2, int) and b2 == 0:
                        dve.wait_ge(s["res_set"], 1)
                    ln1.wait()
                    ln1.inc(v.tensor_tensor(y1[:], att1[:].rearrange("p (q h) d -> p q (h d)", q=QT),
                                            tiles_of(xres, b2), ALU.add))
                if on(b3):
                    xmax_tile(b3, 1)
                if on(b2):
                    stats(ln1, y1, st1)
                if on(b4):
                    norm2_add(ln2, b4)
                if on(b2):
                    aggregate(ln1, st1, mv1)
                if on(b4):
                    stats(ln2, y2, st2)
                if on(b3):
                    xmax_tile(b3, 2)
                if on(b4):
                    aggregate(ln2, st2, mv2)
                if on(b2):
                    dve.wait_ge(s["rstd1"], 2 * (b2 + 1))
                    apply_norm(ln1, x1, b2, y1, mv1, rs1)
                if on(b3):
                    xmax_tile(b3, 3)
                    dve.wait_ge(s["xmax_done"], 4 * (b3 + 1))
                    split_max("m2_split", b3, mx2, mneg2, H2)
                    if on(b4):
                        dve.wait_ge(s["pv2_done"], 2 * (b4 + 1))
                    else:
                        dve.wait_ge(s["v2_kept"], 4)
                        dve.wait_ge(s["ones_set"], 2)
                    v.tensor_copy(k2cur[:], k2S[:, :, bass.ds(b3 * SK, SK)]).then_inc(s["k2cur_set"], 1)
                    v.tensor_copy(v2cur[:], v2aug[:, b3, :, :]).then_inc(s["v2cur_set"], 1)
                if on(b4):
                    norm2_apply(ln2, b4)

            pipeline(dve, step)

            lins = [ps_exp[1], ps_pv]
            down = [ps_max[0], ps_max[1]]

            def accumulate(g, e):
                dve.wait_ge(s["down_ready"], g * NE + e + 1)
                if not (isinstance(g, int) and e == 0):
                    dve.wait_ge(s["acc_done"], g * NE + e)
                for q in range(GT // P):
                    n = g * (GT // P) + q
                    m = v.scalar_tensor_tensor(acc[:, n, :], down[e % 2][:, q * P:(q + 1) * P], cw[:, n, e:e + 1],
                                               acc[:, n, :], ALU.mult, ALU.add)
                m.then_inc(s["acc_done"], 1)

            def last_norm(g):
                ln3 = Steps(dve, "ln3", LN3_STEPS * g)
                wait_alone(dve, s["acc_done"], NE * (g + 1), s["carrier"])
                for q in range(GQ):
                    ln3.inc(v.bn_stats(st3[:, q, :], acc[:, g * GQ + q, :]))
                ln3.wait()
                for q in range(GQ):
                    ln3.inc(v.bn_aggr(mv3[:, q, :], st3[:, q, :]))
                wait_alone(dve, s["rstd3"], 2 * (g + 1), s["carrier"])
                for q in range(GQ):
                    ln3.inc(v.tensor_scalar(yout[:, g * GQ + q, :], acc[:, g * GQ + q, :], mv3[:, q, 0:1],
                                            rs3[:, q:q + 1], ALU.subtract, ALU.mult))

            def products(g):
                if isinstance(g, int):
                    ln2 = norm2_read(B - 1)
                for e in range(NE):
                    if not (isinstance(g, int) and e < 2):
                        dve.wait_ge(s["down_ready"], g * NE + e - 1)
                    for c in range(CH):
                        dve.wait_ge(s["silu_done"], (g * NE + e) * CH + c + 1)
                        v.tensor_tensor(hid[:, (e % 2) * CH + c, :], silu[:, c, :], lins[c][:], ALU.mult)\
                            .then_inc(s["hid_done"], 1)
                        if isinstance(g, int) and (e, c) == (0, 1):
                            norm2_add(ln2, B - 1)
                            stats(ln2, y2, st2)
                            aggregate(ln2, st2, mv2)
                        if isinstance(g, int) and (e, c) == (1, 0):
                            norm2_apply(ln2, B - 1)
                    if e == 0:
                        dve.wait_ge(s["acc_set"], GT // S * (g + 1))
                    if e >= 1:
                        accumulate(g, e - 1)
                    if isinstance(g, int) and e == 3:
                        route(1)
                    if e == 2 and not isinstance(g, int):
                        last_norm(g - 1)
                accumulate(g, NE - 1)

            products(0)
            with dve.Fori(1, NG) as g:
                products(g)
            last_norm(NG - 1)


def kernel(**inputs):
    import numpy as np
    import concourse.bacc as bacc
    from concourse.bass_utils import run_bass_kernel_spmd

    i = {k: np.asarray(v) for k, v in inputs.items()}
    c = np.ascontiguousarray
    f = np.float32

    def rows(w):
        return w.reshape(2, P, DH1).transpose(1, 0, 2)

    a = {}
    x = i["x"].reshape(B * S, D)
    a["x"] = c(x)
    a["xT"] = c(x.T)
    a["lowV"] = c(np.stack([rows(i["L0_attn_V" + n]) for n in "qkv"], axis=1))
    a["lowU"] = c(np.stack([rows(i["L0_attn_U" + n].transpose(0, 2, 1)) for n in "qkv"], axis=1))
    a["bqk"] = c(np.stack([i["L0_attn_bq"].T.reshape(D), i["L0_attn_bk"].T.reshape(D)], axis=1))
    a["bv1"] = c(i["L0_attn_bv"].reshape(D))
    dh = np.arange(D).reshape(H2, DH2).T.reshape(D)
    a["wx"] = c(np.stack([i["L0_xattn_W" + n][:, dh if n in "qk" else slice(None)] for n in "qkvo"], axis=1))
    a["bx"] = c(np.stack([i["L0_xattn_b" + n][dh if n in "qk" else slice(None)] for n in "qkv"], axis=1))
    a["bo"] = c(i["L0_xattn_bo"])
    a["ctxT"] = c(i["ctx_1024"].reshape(B * SK, D).T)
    a["maskT"] = c(i["mask_SxS2_bk0"].T)
    a["rwT"] = c(i["L0_ffn_router_w"].T)
    a["ebias"] = c(i["L0_ffn_experts_bias"])
    for n in ("", "s"):
        a[n + "w13"] = c(np.stack([i["L0_ffn_" + n + w].transpose(1, 0, 2) for w in ("w1", "w3")], axis=2))
    for n in ("w2", "sw2"):
        w = i["L0_ffn_" + n]
        a[n] = c(w.reshape(w.shape[0], CH, P, D).transpose(2, 0, 1, 3))
    a["ident"] = np.eye(P, dtype=f)
    hm = np.zeros((P, 2, H1), f)
    for p in range(P):
        for ch in range(2):
            hm[p, ch, (ch * P + p) // R1] = 1
    a["headmask"] = hm
    a["onesrow"] = np.full((2, H2 * B * SK // 2), 0x3F803F80, np.uint32).view(f)
    a["iotaE"] = np.tile(np.arange(E, dtype=f), (P, 1))

    nc = bacc.Bacc("TRN2", target_bir_lowering=False, num_devices=1)
    t = {n: nc.dram_tensor("in_" + n, v.shape, mybir.dt.from_np(v.dtype), kind="ExternalInput").ap()
         for n, v in a.items()}
    t["out"] = nc.dram_tensor("out", [B * S, D], F32, kind="ExternalOutput").ap()
    decoder_kernel(nc, t)
    r = run_bass_kernel_spmd(nc, [{"in_" + n: v for n, v in a.items()}], core_ids=[0])
    return r.results[0]["out"].reshape(B, S, D)
```
